# Optimizing a Trainium2 kernel written in Bass

```python
import numpy as np
import jax
import jax.numpy as jnp

def _softmax(x, axis=-1):
    return jax.nn.softmax(x, axis=axis)

def _gelu(x):
    return jax.nn.gelu(x, approximate=True)

def _silu(x):
    return jax.nn.silu(x)

def _sigmoid(x):
    return jax.nn.sigmoid(x)

def _layernorm(x, axis=-1, eps=1e-05):
    m = jnp.mean(x, axis=axis, keepdims=True)
    v = jnp.var(x, axis=axis, keepdims=True)
    return (x - m) / jnp.sqrt(v + eps)

def _scatter_add(tgt, idx, src, axis=0):
    return tgt.at[idx].add(src)

def _segment_sum(src, seg, n):
    return jax.ops.segment_sum(src, seg, n)
kernel_name = 'mk_adaln_d1_jaxref_r8_2e1f4e'

def setup_inputs(seed: int=0):
    np.random.seed(seed)
    _w = jnp.asarray

    def _L0_attn_setup():
        import jax, jax.numpy as jnp
        import numpy as np
        ROPE_BASE = 1250
        B, L, D, NH = (2, 256, 128, 16)
        HD = D // NH

        def apply_rope(inputs, positions, base_frequency):
            head_dim = inputs.shape[-1]
            fraction = 2 * jnp.arange(0, head_dim // 2) / head_dim
            timescale = base_frequency ** fraction
            sinusoid = positions[..., None] / timescale[None, None, :]
            sinusoid = sinusoid[..., None, :]
            sin, cos = (jnp.sin(sinusoid), jnp.cos(sinusoid))
            first, second = jnp.split(inputs, 2, axis=-1)
            out = jnp.concatenate([first * cos - second * sin, second * cos + first * sin], axis=-1)
            return out.astype(inputs.dtype)
        key = jax.random.key(seed)
        ks = jax.random.split(key, 5)
        s = 0.02
        return {'x': jax.random.normal(ks[0], (B, L, D), jnp.float32), 'wq_w': jax.random.normal(ks[1], (D, D), jnp.float32) * s, 'wq_b': jnp.zeros((D,), jnp.float32), 'wk_w': jax.random.normal(ks[2], (D, D), jnp.float32) * s, 'wk_b': jnp.zeros((D,), jnp.float32), 'wv_w': jax.random.normal(ks[3], (D, D), jnp.float32) * s, 'wv_b': jnp.zeros((D,), jnp.float32), 'wo_w': jax.random.normal(ks[4], (D, D), jnp.float32) * s, 'wo_b': jnp.zeros((D,), jnp.float32)}
    _L0_attn_in = _L0_attn_setup()

    def _L0_ffn_setup():
        import jax, jax.numpy as jnp
        import numpy as np
        TOP_K = 2
        key = jax.random.key(seed)
        k0, k1, k2, k3, k4 = jax.random.split(key, 5)
        B, S, H, I, E = (1, 512, 128, 256, 8)
        hidden_states = jax.random.normal(k0, (B, S, H), dtype=jnp.float32)
        wg = jax.random.normal(k1, (E, H), dtype=jnp.float32) * 0.02
        w1 = jax.random.normal(k2, (E, I, H), dtype=jnp.float32) * 0.02
        w3 = jax.random.normal(k3, (E, I, H), dtype=jnp.float32) * 0.02
        w2 = jax.random.normal(k4, (E, H, I), dtype=jnp.float32) * 0.02
        return {'hidden_states': hidden_states, 'wg': wg, 'w1': w1, 'w3': w3, 'w2': w2}
    _L0_ffn_in = _L0_ffn_setup()
    _L0_c = _w((lambda *s: np.random.randn(*s).astype(np.float32) * 0.05)(4, 128))
    _L0_wmod = _w((lambda *s: np.random.randn(*s).astype(np.float32) * 0.05)(128, 6 * 128) * 128 ** (-0.5))
    _d = {'L0_attn_x': _L0_attn_in['x'], 'L0_attn_wq_w': _L0_attn_in['wq_w'], 'L0_attn_wq_b': _L0_attn_in['wq_b'], 'L0_attn_wk_w': _L0_attn_in['wk_w'], 'L0_attn_wk_b': _L0_attn_in['wk_b'], 'L0_attn_wv_w': _L0_attn_in['wv_w'], 'L0_attn_wv_b': _L0_attn_in['wv_b'], 'L0_attn_wo_w': _L0_attn_in['wo_w'], 'L0_attn_wo_b': _L0_attn_in['wo_b'], 'L0_ffn_wg': _L0_ffn_in['wg'], 'L0_ffn_w1': _L0_ffn_in['w1'], 'L0_ffn_w3': _L0_ffn_in['w3'], 'L0_ffn_w2': _L0_ffn_in['w2'], 'L0_c': _L0_c, 'L0_wmod': _L0_wmod}
    _x0 = _d['L0_attn_x']
    _d['L0_attn_x'] = jax.random.normal(jax.random.fold_in(jax.random.key(seed), 1), (4, 1024, 128), dtype=_x0.dtype)
    del _x0
    return _d

def reference(L0_attn_x, L0_attn_wq_w, L0_attn_wq_b, L0_attn_wk_w, L0_attn_wk_b, L0_attn_wv_w, L0_attn_wv_b, L0_attn_wo_w, L0_attn_wo_b, L0_ffn_wg, L0_ffn_w1, L0_ffn_w3, L0_ffn_w2, L0_c, L0_wmod):

    def _L0_attn_ref(x, wq_w, wq_b, wk_w, wk_b, wv_w, wv_b, wo_w, wo_b):
        import jax, jax.numpy as jnp
        import numpy as np
        ROPE_BASE = 1250
        B, L, D, NH = (2, 256, 128, 16)
        HD = D // NH

        def apply_rope(inputs, positions, base_frequency):
            head_dim = inputs.shape[-1]
            fraction = 2 * jnp.arange(0, head_dim // 2) / head_dim
            timescale = base_frequency ** fraction
            sinusoid = positions[..., None] / timescale[None, None, :]
            sinusoid = sinusoid[..., None, :]
            sin, cos = (jnp.sin(sinusoid), jnp.cos(sinusoid))
            first, second = jnp.split(inputs, 2, axis=-1)
            out = jnp.concatenate([first * cos - second * sin, second * cos + first * sin], axis=-1)
            return out.astype(inputs.dtype)
        b, l, _ = x.shape
        q = (x @ wq_w + wq_b).reshape(b, l, NH, HD)
        k = (x @ wk_w + wk_b).reshape(b, l, NH, HD)
        v = (x @ wv_w + wv_b).reshape(b, l, NH, HD)
        pos = jnp.arange(l)
        q = apply_rope(q, pos, ROPE_BASE)
        k = apply_rope(k, pos, ROPE_BASE)
        q = q.transpose(0, 2, 1, 3)
        k = k.transpose(0, 2, 1, 3)
        v = v.transpose(0, 2, 1, 3)
        scale = jnp.sqrt(jnp.asarray(HD, q.dtype))
        scores = jnp.einsum('bnqh,bnkh->bnqk', q, k) / scale
        causal = jnp.tril(jnp.ones((l, l), bool))
        scores = jnp.where(causal, scores, jnp.finfo(scores.dtype).min)
        attn = jax.nn.softmax(scores, axis=-1)
        ctx = jnp.einsum('bnqk,bnkh->bnqh', attn, v)
        ctx = ctx.transpose(0, 2, 1, 3).reshape(b, l, D)
        return ctx @ wo_w + wo_b

    def _L0_ffn_ref(hidden_states, wg, w1, w3, w2):
        import jax, jax.numpy as jnp
        import numpy as np
        TOP_K = 2
        orig_shape = hidden_states.shape
        H = orig_shape[-1]
        E = wg.shape[0]
        x = hidden_states.reshape(-1, H)
        router_logits = x @ wg.T
        probs = jax.nn.softmax(router_logits, axis=-1)
        topk_w, topk_idx = jax.lax.top_k(probs, TOP_K)
        topk_w = topk_w / jnp.sum(topk_w, axis=-1, keepdims=True)
        expert_w = jnp.sum(jax.nn.one_hot(topk_idx, E, dtype=x.dtype) * topk_w[..., None], axis=1)
        h1 = jnp.einsum('th,eih->tei', x, w1)
        h3 = jnp.einsum('th,eih->tei', x, w3)
        y = jnp.einsum('tei,ehi->teh', jax.nn.silu(h1) * h3, w2)
        out = jnp.einsum('te,teh->th', expert_w, y)
        return out.reshape(orig_shape)
    x = L0_attn_x
    mod = (_silu(L0_c) @ L0_wmod).reshape(L0_c.shape[0], 6, 1, -1)
    sa, ca, ga, sb, cb, gb = (mod[:, 0], mod[:, 1], mod[:, 2], mod[:, 3], mod[:, 4], mod[:, 5])
    ga = (2 * (ga >= 0) - 1) * jnp.maximum(jnp.abs(ga), 0.25)
    gb = (2 * (gb >= 0) - 1) * jnp.maximum(jnp.abs(gb), 0.25)
    h = _layernorm(x, axis=-1) * (1 + ca) + sa
    x = x + ga * _L0_attn_ref(h, L0_attn_wq_w, L0_attn_wq_b, L0_attn_wk_w, L0_attn_wk_b, L0_attn_wv_w, L0_attn_wv_b, L0_attn_wo_w, L0_attn_wo_b)
    h = _layernorm(x, axis=-1) * (1 + cb) + sb
    x = x + gb * _L0_ffn_ref(h, L0_ffn_wg, L0_ffn_w1, L0_ffn_w3, L0_ffn_w2)
    return x

_drawn_inputs = setup_inputs


def setup_inputs(seed=0):
    import zlib

    import numpy as np

    out = dict(_drawn_inputs(seed))
    spreads = {'L0_attn_wq_b': (0.0, 0.8),
     'L0_attn_wk_b': (0.0, 0.8),
     'L0_attn_wv_b': (0.0, 0.8),
     'L0_attn_wo_b': (0.0, 0.303)}
    factors = {'L0_attn_wq_w': 8.0,
     'L0_attn_wk_w': 8.0,
     'L0_attn_wv_w': 8.0,
     'L0_attn_wo_w': 8.0,
     'L0_ffn_wg': 8.0,
     'L0_ffn_w1': 8.0,
     'L0_ffn_w3': 8.0,
     'L0_ffn_w2': 8.0}
    for name, (base, spread) in spreads.items():
        noise = np.random.default_rng([zlib.crc32(name.encode()), seed]).standard_normal(out[name].shape)
        drawn = base * np.exp(spread * noise) if base else spread * noise
        out[name] = jnp.asarray(drawn.astype(out[name].dtype))
    for name, factor in factors.items():
        out[name] = (out[name] * factor).astype(out[name].dtype)
    return out
```

```python
from contextlib import ExitStack

import numpy as np
import concourse.bass as bass
from concourse import mybir

F32 = mybir.dt.float32
F32R = mybir.dt.float32r
BF16 = mybir.dt.bfloat16
ALU = mybir.AluOpType
ACT = mybir.ActivationFunctionType
X = mybir.AxisListType.X
ds = bass.ds

P = 128
B, L, D = 4, 1024, 128
NH, HD = 16, 8
E, I = 8, 256
CH = 512
NCH = B * L // CH
NB = L // P
CB = CH // P
G = 4
UNITS = B * NH // G
NF = E * I // P
SR = HD * 4
ROWS = SR + 3
STEPS = 2 * (CB + NB)
BUFS = 3
MASKED = -3.0e38
EPS = 1e-5
START = 1
SA, CA, GA, SB, CB_, GB = range(6)

B_SCORES = (0, 2)
B_CTX, B_MAX, B_MISC = 4, 5, 7


def key_steps():
    out = []
    for c in range(2):
        for kb in range(CB * (c + 1)):
            out.append((c, kb, max(0, kb - CB * c) * P))
    return out


KEYS = key_steps()
DIAGONAL = [q for q, (c, kb, _) in enumerate(KEYS) if kb >= CB * c]


def max_pieces():
    out = []
    for qb in range(CB):
        w = (qb + 1) * P
        for pairs in ([(0, 1)] if 2 * w <= CH else [(0,), (1,)]):
            out += [(j, pairs, qb, 0, w, 0) for j in range(2)]
    first = len(out)
    for qb in range(CB, NB):
        w = (qb - CB + 1) * P
        for pairs in ([(0, 1)] if 2 * w <= CH else [(0,), (1,)]):
            out += [(j, pairs, qb, CH, w, 1) for j in range(2)]
        out += [(j, (p,), qb, 0, CH, 0) for p in range(2) for j in range(2)]
    return out, first


PIECES, FIRST_CHUNK_PIECES = max_pieces()
NP = len(PIECES)
NEG0_AT = FIRST_CHUNK_PIECES + 4
NEG0_READ_AT = NEG0_AT + 2
CTX0_AT = 2 * CB + 5


def pieces_before():
    cols = [2 * (CH - off) for c, kb, off in KEYS for _ in range(2)]
    total, done, m, mcols, out = sum(cols), 0, 0, 0, []
    for w in cols:
        done += w
        while m < NP and mcols < done:
            mcols += PIECES[m][4] * len(PIECES[m][1])
            m += 1
        out.append(m)
    out[-1] = NP
    return out


BEFORE = pieces_before()


def build(nc, x, w_in5, cols_in, bv, wo, wgT, w1T, w3T, w2T, cT, wmod,
          rope, ident, mask_up, before, out):
    q_dram = nc.dram_tensor("q_split", (UNITS, 2, 2, 2, HD, L), F32R, kind="Internal").ap()
    k_dram = nc.dram_tensor("k_split", (UNITS, 2, 2, 3, HD, L), F32R, kind="Internal").ap()
    ew_dram = nc.dram_tensor("expert_w", (E, B * L), F32, kind="Internal").ap()

    with ExitStack() as ctx:
        def sb(name, shape, dt=F32, where=ctx):
            return where.enter_context(nc.sbuf_tensor(name, shape, dt))

        def sem(name):
            return ctx.enter_context(nc.semaphore(name))

        ps = ctx.enter_context(nc.psum_tensor("ps", [P, 8, CH], F32))

        x_sb = sb("x_sb", [P, B * NB, D])
        wo_sb, identf = sb("wo_sb", [P, D]), sb("identf", [P, P])
        identb = sb("identb", [P, P], BF16)
        maskb = sb("maskb", [P, P], BF16)
        beforej = sb("beforej", [P, E, E])
        wg_sb = sb("wg_sb", [P, E])
        cols = sb("cols", [P, 5])
        c_sb = sb("c_sb", [P, B])
        silu_c = sb("silu_c", [P, B])
        mod = sb("mod", [P, 6, B])
        gate_abs, gate_sign = sb("gate_abs", [P, B]), sb("gate_sign", [P, B])
        mod_now, mod_now2 = sb("mod_now", [P, 6]), sb("mod_now2", [P, 6])
        gb_chunk, gb_now = sb("gb_chunk", [P, B, 2]), sb("gb_now", [P, 1])
        power = sb("power", [P, NB])
        stats, moments = sb("stats", [P, NB, 6]), sb("moments", [P, NB, 2])
        var_eps, rstd = sb("var_eps", [P, NB]), sb("rstd", [P, NB])
        logits = sb("logits", [P, B * NB, E])
        v_all = sb("v_all", [P, UNITS, NB, G * HD])
        ctx_all = sb("ctx_all", [P, UNITS, NB, G * HD])

        def region(*tenants):
            out, sizes = {}, []
            for t in tenants:
                stack = ExitStack()
                sizes.append((sum(int(np.prod(s[1:])) * (2 if d == BF16 else 4) for _, s, d in t), t))
                for name, shape, dt in t:
                    out[name] = sb(name, shape, dt, stack)
                stack.close()
            most = max(s for s, _ in sizes)
            sb(f"region_{len(regions)}", [P, most // 4])
            regions.append(most)
            return out

        regions = []
        r1 = region([(f"{n}{k}", [P, 2, L], F32R) for n in "qk" for k in range(BUFS)],
                    [(f"{n}_{h}", [P, E * I], F32R) for n in ("w1", "w3", "w2") for h in ("hi", "lo")])
        q_s, k_s = [r1[f"q{k}"] for k in range(BUFS)], [r1[f"k{k}"] for k in range(BUFS)]
        w1_hi, w1_lo, w3_hi, w3_lo, w2_hi, w2_lo = (r1[f"{n}_{h}"] for n in ("w1", "w3", "w2") for h in ("hi", "lo"))
        r2 = region([("probs", [P, BUFS, G, CH], F32), ("v_unit", [P, BUFS, NB, G, 32], F32)],
                    [("h2_hi", [P, B * L], F32R), ("h2_lo", [P, B * L], F32R),
                     ("y_sb", [P, CH], F32), ("o_sb", [P, CB, D], F32)])
        probs, v_unit, h2_hi, h2_lo, y_sb, o_sb = (
            r2[n] for n in ("probs", "v_unit", "h2_hi", "h2_lo", "y_sb", "o_sb"))
        r3 = region(
            [("rope_sb", [P, 2, L], F32), ("w_proj", [P, 5, D], F32), ("bv_sb", [P, D], F32), ("wmod_sb", [P, 6 * D], F32), ("mask_f", [P, P], F32),
             ("xn", [P, 2, CB, D], F32), ("h_t", [P, 2, CH], F32), ("rot1", [P, 2, CH], F32),
             ("rot2", [P, 2, CH], F32), ("qk_f", [P, 2, 2, CH], F32), ("qk_hi", [P, 2, 2, CH], F32R),
             ("qk_lo", [P, 2, 2, CH], F32R)],
            [("w_in", [P, 3, E * I], F32), ("ctx_st", [P, 2, CB, D], F32), ("ctx_t", [P, 2, CH], F32),
             ("att_t", [P, 2, CH], F32), ("xn2", [P, 2, CB, D], F32), ("h2_t", [P, 2, CH], F32),
             ("rank3", [P, B * NB, E, E], F32)],
            [("wb", [P, E, CH], F32), ("s_f", [P, 4, CH], F32), ("g_f", [P, 4, CH], F32), ("gw_f", [P, 4, CH], F32),
             ("g_hi", [P, 4, CH], F32R), ("g_lo", [P, 4, CH], F32R)])
        rope_sb, w_proj, bv_sb, wmod_sb, mask_f, xn, h_t, rot1, rot2, qk_f, qk_hi, qk_lo = (
            r3[n] for n in ("rope_sb", "w_proj", "bv_sb", "wmod_sb", "mask_f", "xn", "h_t", "rot1", "rot2", "qk_f", "qk_hi", "qk_lo"))
        w_in, ctx_st, ctx_t, att_t, xn2, h2_t, rank3 = (
            r3[n] for n in ("w_in", "ctx_st", "ctx_t", "att_t", "xn2", "h2_t", "rank3"))
        wb, s_f, g_f, gw_f, g_hi, g_lo = (r3[n] for n in ("wb", "s_f", "g_f", "gw_f", "g_hi", "g_lo"))
        neg = sb("neg", [P, 2, 2, 2, CB])
        negm = sb("negm", [P, 2, 2, CB])
        neg_split = sb("neg_split", [P, 2, CB, 2, 2, 2], F32R)
        neg_t = sb("neg_t", [8, 2, CH], F32R)
        cat = sb("cat", [P, 2, CH])
        rsum = sb("rsum", [P, CB, G])
        eqs = sb("eqs", [P, B * NB, E])
        sel, lmax = sb("sel", [P, B * NB, E]), sb("lmax", [P, B * NB])
        ew, ez = sb("ew", [P, B * NB, E]), sb("ez", [P, B * NB])
        ew_t = sb("ew_t", [P, 2, P])

        names = """waited mask_set w_loaded c_loaded x_loaded silu_c_done mod_mm mod_chain mod_done const_set
            ln_stats ln_moments ln_eps rstd_ready mod_cur xn_ready xt_done h_ready v_proj qk_proj rope_read
            qkf_ready hi_ready lo_ready v_evac scratch_written rows_set
            score_banks_free scores_ready probs_given_back mask_done v_staged units_done pieces_ready
            reduced neg_min neg_hi neg_lo neg_tp neg_evac ctx_evac ctx_tp sums_done ctx_finished
            ctx_staged ctx2_tp ctx2_evac att_mm att_evac att_tp x2_ready logit_mm logit_read h2hi_ready
            h2lo_ready w_in_loaded whi_ready wlo_ready route_chain lmax_sub ex_ready ewt_mm ewt_ready ew_written
            h_banks silu_done g_done gw_done ghi_done glo_done y_mm y_evac y_tp o_ready gb_cur""".split()
        S = {n: sem(n) for n in names}
        qk_loaded = [sem(f"qk_loaded{k}") for k in range(BUFS)]
        neg_loaded = [sem(f"neg_loaded{c}") for c in range(2)]
        wb_loaded = [sem(f"wb_loaded{e}") for e in range(E)]
        out_written = sem("out_written")

        x_v = x.rearrange("b (n p) d -> p b n d", p=P)
        out_v = out.rearrange("b (n p) d -> p (b n) d", p=P)
        block = ctx.enter_context(nc.Block())
        UNIT_DMAS, NEG_DMAS = 8, 4
        N_WEIGHT_DMAS = 9

        def wait_alone(eng, semaphore, value):
            eng.wait_ge(semaphore, value)
            eng.sem_inc(S["waited"], 1)

        def norm_stats(dve, n0, done):
            for j in range(NB):
                last = nc.vector.bn_stats(stats[:, j, :], x_sb[:, ds(n0 + j, 1), :].rearrange("p a d -> p (a d)"))
            last.then_inc(S["ln_stats"], 1)
            wait_alone(dve, S["ln_stats"], done)
            for j in range(NB):
                last = nc.vector.bn_aggr(moments[:, j, :], stats[:, j, :])
            last.then_inc(S["ln_moments"], 1)

        def norm_rows(dve, n0, half, dst):
            for a in range(CB):
                j = CB * half + a
                last = nc.vector.tensor_scalar(
                    dst[:, half, a, :], x_sb[:, ds(n0 + j, 1), :].rearrange("p a d -> p (a d)"),
                    moments[:, j, 0:1], rstd[:, j:j + 1], ALU.subtract, ALU.mult)
            last.then_inc(S["xn_ready"], 1)

        def rstd_of(pool, done):
            wait_alone(pool, S["ln_moments"], done)
            nc.gpsimd.tensor_scalar(var_eps[:], moments[:, :, 1], EPS, None, ALU.add).then_inc(S["ln_eps"], 1)
            pool.wait_ge(S["ln_eps"], done)
            nc.gpsimd.tensor_tensor(rstd[:], var_eps[:], power[:], ALU.pow).then_inc(S["rstd_ready"], 1)

        from_start = [S[n] for n in """h_ready xt_done qk_proj qkf_ready lo_ready scratch_written v_evac
            rope_read ctx2_tp att_mm h2lo_ready logit_mm logit_read att_evac att_tp x2_ready ctx_tp
            ctx_finished ctx_evac y_evac o_ready""".split()] + neg_loaded + [out_written]

        @block.sync
        def _(sp):
            for semaphore in from_start:
                sp.sem_inc(semaphore, START)
            with sp.Fori(0, B) as b:
                sp.dma_start(x_sb[:, ds(b * NB, NB), :],
                             x_v[:, ds(b, 1)].rearrange("p a n d -> p (a n) d")).then_inc(S["x_loaded"], 16)
                wait_alone(sp, S["x_loaded"], 16 * b + 16)
            with sp.Fori(0, B) as b:
                for k in range(2):
                    cs = slice(k * CH, (k + 1) * CH)
                    for s in range(2):
                        n = 4 * b + (2 * k + s + 1)
                        dst = (q_dram, k_dram)[s][ds(4 * b, 4)].rearrange("g p j h d t -> (g p j) h d t")
                        sp.wait_ge(S["hi_ready"], n)
                        for slot in ((0,), (0, 2))[s]:
                            sp.dma_start(dst[:, slot, :, cs].bitcast(F32), qk_hi[:, s, k, :].bitcast(F32)
                                         ).then_inc(S["scratch_written"], 16)
                        sp.wait_ge(S["lo_ready"], n + START)
                        sp.dma_start(dst[:, 1, :, cs].bitcast(F32), qk_lo[:, s, k, :].bitcast(F32)
                                     ).then_inc(S["scratch_written"], 16)
            sp.wait_ge(S["scratch_written"], 16 * 10 * B + START)

            def load_unit(w, k):
                sp.wait_ge(S["units_done"], w + 1)
                for j in range(2):
                    for half in range(2):
                        rows = slice(64 * j + 2 * HD * half, 64 * j + 2 * HD * (half + 1))
                        q_src = q_dram[ds(w, 1), :, j].rearrange("a p h d t -> (a h d) p t")
                        k_src = k_dram[ds(w, 1), :, j, half:half + 2].rearrange("a p h d t -> (a h d) p t")
                        sp.dma_start(q_s[k][rows, :, :].bitcast(F32), q_src.bitcast(F32)).then_inc(qk_loaded[k], 16)
                        sp.dma_start(k_s[k][rows, :, :].bitcast(F32), k_src.bitcast(F32)).then_inc(qk_loaded[k], 16)

            def load_neg(u, k, c):
                sp.wait_ge(S["neg_evac"], 2 * u + (c + 1))
                for p in range(2):
                    for j in range(2):
                        r = 4 * p + 2 * j
                        sp.dma_start(q_s[k][64 * j + SR + 1:64 * j + SR + 3, p, c * CH:(c + 1) * CH].bitcast(F32),
                                     neg_t[r:r + 2, c, :].bitcast(F32)).then_inc(neg_loaded[c], 16)

            sp.wait_ge(S["rows_set"], 1)
            load_unit(0, 0)
            for n, src in enumerate((w1T, w3T, w2T)):
                sp.dma_start(w_in[:, n, :], src).then_inc(S["w_in_loaded"], 16)
            with sp.Fori(0, (UNITS - 1) // BUFS) as t:
                for k in range(BUFS):
                    load_unit(BUFS * t + (k + 1), (k + 1) % BUFS)
                    load_neg(BUFS * t + k, k, 0)
                    load_neg(BUFS * t + k, k, 1)
            load_neg(UNITS - 1, 0, 0)
            load_neg(UNITS - 1, 0, 1)

            sp.wait_ge(S["ewt_ready"], 1)
            for half in range(2):
                for n in range(NB * 2):
                    t0 = (half * 2 * NB + n) * P
                    sp.dma_start(ew_dram[:, t0:t0 + P], ew_t[n * E:(n + 1) * E, half, :]).then_inc(S["ew_written"], 16)
            sp.wait_ge(S["ew_written"], 16 * B * NB)
            sp.wait_ge(S["wlo_ready"], B)

            def load_wb(i, e):
                sp.dma_start(wb[:, e, :], ew_dram[e, ds(i * CH, CH)].partition_broadcast(P)).then_inc(wb_loaded[e], 16)

            def store(i):
                sp.wait_ge(S["o_ready"], i + 1 + START)
                sp.dma_start(out_v[:, ds(CB * i, CB), :], o_sb[:]).then_inc(out_written, 16)

            for e in range(E):
                load_wb(0, e)
            with sp.Fori(0, NCH - 1) as i:
                for e in range(E):
                    sp.wait_ge(S["gw_done"], NF * i + (2 * e + 2))
                    load_wb(i + 1, e)
                store(i)
            store(NCH - 1)
            sp.wait_ge(out_written, 16 * NCH + START)

        @block.gpsimd
        def _(pool):
            nc.gpsimd.memset(power[:], -0.5).then_inc(S["const_set"], 1)
            nc.gpsimd.memset(v_unit[:], 0.0).then_inc(S["const_set"], 1)
            pool.wait_ge(S["const_set"], 2)
            nc.gpsimd.memset(v_unit[:, :, :, :, HD:HD + 1], 1.0).then_inc(S["const_set"], 1)

            with pool.Fori(0, B) as b:
                rstd_of(pool, b + 1)
                for k in range(2):
                    for s in range(2):
                        n = 4 * b + (2 * k + s + 1)
                        pool.wait_ge(S["rope_read"], n + START)
                        pool.wait_ge(S["lo_ready"], 4 * b + START)
                        nc.gpsimd.tensor_tensor(qk_f[:, s, k, :], rot1[:, s, :], rot2[:, s, :], ALU.add
                                                ).then_inc(S["qkf_ready"], 1)

            def stage_v(w, k):
                pool.wait_ge(S["units_done"], w + 1)
                nc.gpsimd.tensor_copy(
                    v_unit[:, k, :, :, 0:HD],
                    v_all[:, ds(w, 1)].rearrange("p a n (h d) -> p (a n) h d", h=G)).then_inc(S["v_staged"], 1)

            def mask_diagonals(u):
                for n, q in enumerate(DIAGONAL):
                    off = KEYS[q][2]
                    wait_alone(pool, S["score_banks_free"], STEPS * u + (2 * q + 4))
                    tile = probs[:, q % BUFS, :, off:off + P]
                    nc.gpsimd.affine_select(out=tile, in_=tile, compare_op=ALU.is_ge, fill=0.0, base=0,
                                            pattern=[[0, G], [1, P]], channel_multiplier=-1
                                            ).then_inc(S["mask_done"], 1)

            pool.wait_ge(S["v_evac"], NCH + START)
            pool.wait_ge(S["const_set"], 3)
            stage_v(0, 0)
            with pool.Fori(0, (UNITS - 1) // BUFS) as t:
                for k in range(BUFS):
                    stage_v(BUFS * t + (k + 1), (k + 1) % BUFS)
                    mask_diagonals(BUFS * t + k)
            mask_diagonals(UNITS - 1)

            pool.wait_ge(S["ctx_finished"], 2 * UNITS + START)
            pool.wait_ge(S["w_in_loaded"], 48)
            with pool.Fori(0, B) as b:
                for k in range(2):
                    pool.wait_ge(S["ctx2_tp"], 2 * b + START)
                    for g in range(NH // G):
                        last = nc.gpsimd.tensor_copy(
                            ctx_st[:, k, :, g * G * HD:(g + 1) * G * HD],
                            ctx_all[:, ds(4 * b + g, 1), CB * k:CB * (k + 1), :].rearrange("p a n d -> p (a n) d"))
                    last.then_inc(S["ctx_staged"], 1)
                rstd_of(pool, B + b + 1)
                for k in range(2):
                    pool.wait_ge(S["h2hi_ready"], 2 * b + (k + 1))
                    nc.gpsimd.tensor_tensor(h2_lo[:, ds((2 * b + k) * CH, CH)], h2_t[:, k, :],
                                            h2_hi[:, ds((2 * b + k) * CH, CH)].bitcast(F32), ALU.subtract
                                            ).then_inc(S["h2lo_ready"], 1)
                pool.wait_ge(S["whi_ready"], b + 1)
                for n, (hi, lo) in enumerate(((w1_hi, w1_lo), (w3_hi, w3_lo), (w2_hi, w2_lo))):
                    last = nc.gpsimd.tensor_tensor(lo[:, ds(b * CH, CH)], w_in[:, n, ds(b * CH, CH)],
                                                   hi[:, ds(b * CH, CH)].bitcast(F32), ALU.subtract)
                last.then_inc(S["wlo_ready"], 1)

            with pool.Fori(0, NCH) as i:
                for f in range(NF):
                    if f % 2 == 0:
                        pool.wait_ge(wb_loaded[f // 2], 16 * i + 16)
                    pool.wait_ge(S["g_done"], NF * i + (f + 1))
                    nc.gpsimd.tensor_tensor(gw_f[:, f % 4, :], g_f[:, f % 4, :], wb[:, f // 2, :], ALU.mult
                                            ).then_inc(S["gw_done"], 1)

        @block.scalar
        def _(act):
            act.dma_start(c_sb[:], cT).then_inc(S["c_loaded"], 16)
            act.dma_start(wmod_sb[:], wmod).then_inc(S["c_loaded"], 16)
            for dst, src in ((w_proj[:], w_in5), (cols[:], cols_in), (identf[:], ident), (mask_f[:], mask_up),
                             (rope_sb[:], rope), (wo_sb[:], wo), (wg_sb[:], wgT),
                             (bv_sb[:], bv.partition_broadcast(P))):
                act.dma_start(dst, src).then_inc(S["w_loaded"], 16)
            act.dma_start(beforej[:], before).then_inc(S["w_loaded"], 16)
            act.sem_inc(S["score_banks_free"], 2)
            act.wait_ge(S["c_loaded"], 32)
            nc.scalar.activation(silu_c[:], c_sb[:], ACT.Silu).then_inc(S["silu_c_done"], 1)

            act.wait_ge(S["mod_done"], 1)
            with act.Fori(0, B) as b:
                act.wait_ge(S["mod_cur"], b + 1)
                for k in range(2):
                    act.wait_ge(S["xt_done"], 2 * b + (k + 1) + START)
                    act.wait_ge(S["qk_proj"], 4 * b + START)
                    nc.scalar.activation(h_t[:, k, :], ps[:, k, :], ACT.Identity, bias=mod_now[:, SA:SA + 1],
                                         scale=mod_now[:, CA:CA + 1]).then_inc(S["h_ready"], 1)
                for k in range(2):
                    for s in range(2):
                        act.wait_ge(S["qkf_ready"], 4 * b + (2 * k + s + 1) + START)
                        act.wait_ge(S["scratch_written"], 160 * b + START)
                        nc.scalar.activation(qk_hi[:, s, k, :], qk_f[:, s, k, :], ACT.Copy
                                             ).then_inc(S["hi_ready"], 1)

            def exps(u):
                for n in range(STEPS):
                    q, p = divmod(n, 2)
                    off = KEYS[q][2]
                    bank = B_SCORES[n % 2]
                    act.wait_ge(S["scores_ready"], STEPS * u + (n + 1))
                    if p == 0:
                        act.wait_ge(S["probs_given_back"], len(KEYS) * u + (q + 1))
                    nc.scalar.activation(probs[:, q % BUFS, 2 * p:2 * p + 2, off:], ps[:, bank:bank + 2, off:],
                                         ACT.Exp, scale=float(HD) ** -0.5).then_inc(S["score_banks_free"], 1)
                    if n in (2 * CB + 2, STEPS - 1):
                        c = int(n == STEPS - 1)
                        act.wait_ge(S["probs_given_back"], len(KEYS) * u + (BUFS + (CB, len(KEYS))[c]))
                        act.wait_ge(S["ctx_tp"], 2 * u + START)
                        nc.scalar.activation(cat[:, c, :], ps[:, B_CTX, :], ACT.Copy).then_inc(S["ctx_evac"], 1)

            with act.Fori(0, (UNITS - 1) // BUFS) as t:
                for k in range(BUFS):
                    exps(BUFS * t + k)
            exps(UNITS - 1)

            act.wait_ge(S["w_in_loaded"], 48)
            act.wait_ge(S["ctx_finished"], 2 * UNITS + START)
            with act.Fori(0, B) as b:
                for k in range(2):
                    act.wait_ge(S["ctx2_tp"], 2 * b + (k + 1) + START)
                    act.wait_ge(S["att_mm"], 2 * b + START)
                    nc.scalar.activation(ctx_t[:, k, :], ps[:, k, :], ACT.Copy).then_inc(S["ctx2_evac"], 1)
                for n, hi in enumerate((w1_hi, w3_hi, w2_hi)):
                    last = nc.scalar.activation(hi[:, ds(b * CH, CH)], w_in[:, n, ds(b * CH, CH)], ACT.Copy)
                last.then_inc(S["whi_ready"], 1)
                act.wait_ge(S["mod_cur"], B + b + 1)
                for k in range(2):
                    act.wait_ge(S["xt_done"], NCH + 2 * b + (k + 1) + START)
                    act.wait_ge(S["h2lo_ready"], 2 * b + START)
                    act.wait_ge(S["logit_mm"], 2 * b + START)
                    nc.scalar.activation(h2_t[:, k, :], ps[:, 6 + k, :], ACT.Identity, bias=mod_now2[:, SB:SB + 1],
                                         scale=mod_now2[:, CB_:CB_ + 1]).then_inc(S["h_ready"], 1)
                for k in range(2):
                    act.wait_ge(S["h_ready"], NCH + 2 * b + (k + 1) + START)
                    nc.scalar.activation(h2_hi[:, ds((2 * b + k) * CH, CH)], h2_t[:, k, :], ACT.Copy
                                         ).then_inc(S["h2hi_ready"], 1)
            act.wait_ge(S["lmax_sub"], 1)
            nc.scalar.activation(ew[:], ew[:], ACT.Exp).then_inc(S["ex_ready"], 1)

            def silu(i, f):
                act.wait_ge(S["h_banks"], NF * i + (f + 1))
                nc.scalar.activation(s_f[:, f % 4, :], ps[:, 2 * (f % 2), :], ACT.Silu).then_inc(S["silu_done"], 1)

            def keep_hi(i, f):
                act.wait_ge(S["gw_done"], NF * i + (f + 1))
                nc.scalar.activation(g_hi[:, f % 4, :], gw_f[:, f % 4, :], ACT.Copy).then_inc(S["ghi_done"], 1)

            def chunk(i, last=False):
                for f in range(NF):
                    if f + 1 < NF:
                        keep_hi(i, f + 1)
                    elif not last:
                        keep_hi(i + 1, 0)
                    if f + 3 < NF:
                        silu(i, f + 3)
                    elif not last:
                        silu(i + 1, f + 3 - NF)

            for f in range(3):
                silu(0, f)
            keep_hi(0, 0)
            with act.Fori(0, NCH - 1) as i:
                chunk(i)
            chunk(NCH - 1, last=True)

        @block.vector
        def _(dve):
            for k in range(BUFS):
                for j in range(2):
                    r = 64 * j + SR
                    nc.vector.memset(q_s[k][r:r + 1, :, :].bitcast(F32), 0.0)
                    last = nc.vector.memset(k_s[k][r:r + 3, :, :].bitcast(F32), 1.0)
            last.then_inc(S["rows_set"], 1)
            dve.wait_ge(S["mod_mm"], 1)
            nc.vector.tensor_copy(mod[:].rearrange("p s b -> p (s b)"), ps[:, 7, 0:6 * B]).then_inc(S["mod_chain"], 1)
            dve.wait_ge(S["mod_chain"], 1)
            for slot in (CA, CB_):
                nc.vector.tensor_scalar(mod[:, slot, :], mod[:, slot, :], 1.0, None, ALU.add)
            n = 1
            for slot in (GA, GB):
                nc.vector.tensor_scalar(gate_sign[:], mod[:, slot, :], 0.0, 2.0, ALU.is_ge, ALU.mult)
                nc.vector.scalar_tensor_tensor(gate_abs[:], mod[:, slot, :], -1.0, mod[:, slot, :], ALU.mult, ALU.max
                                               ).then_inc(S["mod_chain"], 1)
                n += 1
                dve.wait_ge(S["mod_chain"], n)
                nc.vector.tensor_scalar(gate_abs[:], gate_abs[:], 0.25, None, ALU.max).then_inc(S["mod_chain"], 1)
                n += 1
                dve.wait_ge(S["mod_chain"], n)
                nc.vector.scalar_tensor_tensor(mod[:, slot, :], gate_sign[:], -1.0, gate_abs[:], ALU.add, ALU.mult
                                               ).then_inc(S["mod_chain"], 1)
                n += 1
                dve.wait_ge(S["mod_chain"], n)
            for k in range(2):
                last = nc.vector.tensor_copy(gb_chunk[:, :, k], mod[:, GB, :])
            last.then_inc(S["mod_done"], 1)
            dve.wait_ge(S["mod_done"], 1)

            dve.wait_ge(S["w_loaded"], 16 * N_WEIGHT_DMAS)
            nc.vector.tensor_copy(identb[:], identf[:])
            nc.vector.tensor_copy(maskb[:], mask_f[:]).then_inc(S["mask_set"], 1)
            with dve.Fori(0, B) as b:
                wait_alone(dve, S["x_loaded"], 16 * b + 16)
                norm_stats(dve, NB * b, b + 1)
                dve.wait_ge(S["h_ready"], 2 * b + START)
                nc.vector.tensor_copy(mod_now[:], mod[:, :, ds(b, 1)].rearrange("p s a -> p (s a)")
                                      ).then_inc(S["mod_cur"], 1)
                dve.wait_ge(S["rstd_ready"], b + 1)
                dve.wait_ge(S["xt_done"], 2 * b + START)
                for k in range(2):
                    norm_rows(dve, NB * b, k, xn)
                for k in range(2):
                    cs = slice(k * CH, (k + 1) * CH)
                    dve.wait_ge(S["v_proj"], 2 * b + (k + 1))
                    for a in range(CB):
                        last = nc.vector.tensor_tensor(
                            v_all[:, ds(4 * b, 4), CB * k + a, :],
                            ps[:, 6 + k, a * P:(a + 1) * P].rearrange("p (g d) -> p g d", g=4),
                            bv_sb[:].rearrange("p (g d) -> p g d", g=4), ALU.add)
                    last.then_inc(S["v_evac"], 1)
                    for s in range(2):
                        dve.wait_ge(S["qk_proj"], 4 * b + (2 * k + s + 1) + START)
                        dve.wait_ge(S["qkf_ready"], 4 * b + 2 * k + START)
                        nc.vector.scalar_tensor_tensor(rot1[:, s, :], ps[:, 2 + 2 * s, :], cols[:, 2 * s:2 * s + 1],
                                                       rope_sb[:, 0, cs], ALU.add, ALU.mult)
                        nc.vector.scalar_tensor_tensor(rot2[:, s, :], ps[:, 3 + 2 * s, :],
                                                       cols[:, 2 * s + 1:2 * s + 2], rope_sb[:, 1, cs], ALU.add,
                                                       ALU.mult).then_inc(S["rope_read"], 1)
                for k in range(2):
                    for s in range(2):
                        dve.wait_ge(S["hi_ready"], 4 * b + (2 * k + s + 1))
                        dve.wait_ge(S["scratch_written"], 160 * b + START)
                        nc.vector.tensor_tensor(qk_lo[:, s, k, :], qk_f[:, s, k, :], qk_hi[:, s, k, :].bitcast(F32),
                                                ALU.subtract).then_inc(S["lo_ready"], 1)

            def reduce_piece(m, v):
                j, pairs, qb, _, w, part = PIECES[m]
                n = len(pairs)
                dve.wait_ge(S["pieces_ready"], NP * v + (m + 1))
                nc.vector.tensor_reduce(neg[:, part, j, pairs[0]:pairs[-1] + 1, qb % CB],
                                        ps[:, B_MAX + j, 0:n * w].rearrange("p (n w) -> p n w", n=n),
                                        axis=X, op=ALU.max, negate=True).then_inc(S["reduced"], 1)

            def split_neg(c, v):
                dst = neg_split[:, c].rearrange("p q s j h -> p j s q h")
                src = neg[:, 0]
                dve.wait_ge(S["reduced"], NP * v + (NP if c else FIRST_CHUNK_PIECES))
                if c:
                    nc.vector.tensor_tensor(negm[:], neg[:, 0], neg[:, 1], ALU.min).then_inc(S["neg_min"], 1)
                    dve.wait_ge(S["neg_min"], v + 1)
                    src = negm[:]
                for j in range(2):
                    last = nc.vector.tensor_copy(dst[:, j, :, :, 0], src[:, j])
                last.then_inc(S["neg_hi"], 1)
                dve.wait_ge(S["neg_hi"], 2 * v + (c + 1))
                for j in range(2):
                    last = nc.vector.tensor_tensor(dst[:, j, :, :, 1], src[:, j], dst[:, j, :, :, 0].bitcast(F32),
                                                   ALU.subtract)
                last.then_inc(S["neg_lo"], 1)

            def read_neg(c, v):
                dve.wait_ge(S["neg_tp"], 2 * v + (c + 1))
                dve.wait_ge(neg_loaded[c], 16 * NEG_DMAS * v + START)
                nc.vector.tensor_copy(neg_t[:, c, :], ps[0:8, B_MISC, :]).then_inc(S["neg_evac"], 1)

            def finish_context(c, u):
                heads = ps[:, B_MISC, :].rearrange("p (a h r) -> p a h r", a=CB, h=G)
                dve.wait_ge(S["ctx_tp"], 2 * u + (c + 1) + START)
                nc.vector.reciprocal(rsum[:], heads[:, :, :, HD]).then_inc(S["sums_done"], 1)
                dve.wait_ge(S["sums_done"], 2 * u + (c + 1))
                nc.vector.tensor_tensor(
                    ctx_all[:, ds(u, 1), CB * c:CB * (c + 1), :].rearrange("p a n (h d) -> p (a n) h d", h=G),
                    heads[:, :, :, 0:HD], rsum[:].unsqueeze(3).broadcast_to([P, CB, G, HD]), ALU.mult
                ).then_inc(S["ctx_finished"], 1)

            def maxima(v, m):
                if m == FIRST_CHUNK_PIECES:
                    split_neg(0, v)
                if m == NEG0_READ_AT:
                    read_neg(0, v)
                reduce_piece(m, v)

            def unit(u, with_max=True):
                for n in range(STEPS):
                    if with_max:
                        for m in range(BEFORE[n - 1] if n else 0, BEFORE[n]):
                            maxima(u + 1, m)
                    if n == 2:
                        read_neg(1, u)
                    if n == CTX0_AT + 2:
                        finish_context(0, u)
                if with_max:
                    split_neg(1, u + 1)
                finish_context(1, u)

            for m in range(NP):
                maxima(0, m)
            split_neg(1, 0)
            with dve.Fori(0, (UNITS - 1) // BUFS) as t:
                for k in range(BUFS):
                    unit(BUFS * t + k)
            unit(UNITS - 1, with_max=False)

            with dve.Fori(0, B) as b:
                dve.wait_ge(S["h_ready"], NCH + 2 * b + START)
                nc.vector.tensor_copy(mod_now2[:], mod[:, :, ds(b, 1)].rearrange("p s a -> p (s a)")
                                      ).then_inc(S["mod_cur"], 1)
                dve.wait_ge(S["mod_cur"], B + b + 1)
                for k in range(2):
                    dve.wait_ge(S["att_mm"], 2 * b + (k + 1) + START)
                    dve.wait_ge(S["att_tp"], 2 * b + START)
                    nc.vector.tensor_scalar(att_t[:, k, :], ps[:, 2 + k, :], cols[:, 4:5], mod_now2[:, GA:GA + 1],
                                            ALU.add, ALU.mult).then_inc(S["att_evac"], 1)
                for k in range(2):
                    rows = x_sb[:, ds(NB * b + CB * k, CB), :]
                    dve.wait_ge(S["att_tp"], 2 * b + (k + 1) + START)
                    nc.vector.tensor_tensor(rows, ps[:, 4 + k, :].rearrange("p (a d) -> p a d", a=CB), rows, ALU.add
                                            ).then_inc(S["x2_ready"], 1)
                wait_alone(dve, S["x2_ready"], 2 * b + 2 + START)
                norm_stats(dve, NB * b, B + b + 1)
                dve.wait_ge(S["rstd_ready"], B + b + 1)
                dve.wait_ge(S["xt_done"], NCH + 2 * b + START)
                for k in range(2):
                    norm_rows(dve, NB * b, k, xn2)
                for k in range(2):
                    dve.wait_ge(S["logit_mm"], 2 * b + (k + 1) + START)
                    nc.vector.tensor_copy(logits[:, ds(NB * b + CB * k, CB), :],
                                          ps[:, k, 0:CB * E].rearrange("p (a e) -> p a e", a=CB)
                                          ).then_inc(S["logit_read"], 1)

            step = [0]

            def chained(ins):
                step[0] += 1
                ins.then_inc(S["route_chain"], 1)
                dve.wait_ge(S["route_chain"], step[0])

            T = B * NB
            dve.wait_ge(S["logit_read"], NCH + START)
            by_e = logits[:].unsqueeze(3).broadcast_to([P, T, E, E])
            by_j = logits[:].unsqueeze(2).broadcast_to([P, T, E, E])
            chained(nc.vector.reduce_max(lmax[:], logits[:], axis=X))
            nc.vector.tensor_tensor(ew[:], logits[:], lmax[:].unsqueeze(2).broadcast_to([P, T, E]), ALU.subtract
                                    ).then_inc(S["lmax_sub"], 1)
            chained(nc.vector.tensor_tensor(rank3[:], by_j, by_e, ALU.is_equal))
            chained(nc.vector.tensor_tensor(rank3[:], rank3[:], beforej[:].unsqueeze(1).broadcast_to([P, T, E, E]),
                                            ALU.mult))
            chained(nc.vector.reduce_sum(eqs[:], rank3[:], axis=X))
            chained(nc.vector.tensor_tensor(rank3[:], by_j, by_e, ALU.is_gt))
            chained(nc.vector.reduce_sum(sel[:], rank3[:], axis=X))
            chained(nc.vector.tensor_tensor(sel[:], sel[:], eqs[:], ALU.add))
            chained(nc.vector.tensor_scalar(sel[:], sel[:], 1.5, None, ALU.is_lt))
            dve.wait_ge(S["ex_ready"], 1)
            chained(nc.vector.tensor_tensor(ew[:], ew[:], sel[:], ALU.mult))
            chained(nc.vector.reduce_sum(ez[:], ew[:], axis=X))
            chained(nc.vector.reciprocal(ez[:], ez[:]))
            nc.vector.tensor_tensor(sel[:], ew[:], ez[:].unsqueeze(2).broadcast_to([P, T, E]), ALU.mult
                                    ).then_inc(S["route_chain"], 1)
            dve.wait_ge(S["ewt_mm"], 1)
            nc.vector.tensor_copy(ew_t[:], ps[:, 5, 0:2 * P].rearrange("p (h t) -> p h t", h=2)
                                  ).then_inc(S["ewt_ready"], 1)

            def gate(i, f):
                dve.wait_ge(S["silu_done"], NF * i + (f + 1))
                nc.vector.tensor_tensor(g_f[:, f % 4, :], ps[:, 2 * (f % 2) + 1, :], s_f[:, f % 4, :], ALU.mult
                                        ).then_inc(S["g_done"], 1)

            def keep_lo(i, f):
                dve.wait_ge(S["ghi_done"], NF * i + (f + 1))
                nc.vector.tensor_tensor(g_lo[:, f % 4, :], gw_f[:, f % 4, :], g_hi[:, f % 4, :].bitcast(F32),
                                        ALU.subtract).then_inc(S["glo_done"], 1)

            def chunk(i, last=False):
                nc.vector.tensor_copy(gb_now[:], gb_chunk[:].rearrange("p b k -> p (b k)")[:, ds(i, 1)]
                                      ).then_inc(S["gb_cur"], 1)
                for f in range(NF):
                    if f + 1 < NF:
                        keep_lo(i, f + 1)
                    elif not last:
                        keep_lo(i + 1, 0)
                    if f == NF - 1:
                        dve.wait_ge(S["gb_cur"], i + 1)
                        dve.wait_ge(S["y_mm"], i + 1)
                        nc.vector.tensor_scalar(y_sb[:], ps[:, 4, :], gb_now[:, 0:1], None, ALU.mult
                                                ).then_inc(S["y_evac"], 1)
                    if f + 3 < NF:
                        gate(i, f + 3)
                    elif not last:
                        gate(i + 1, f + 3 - NF)
                dve.wait_ge(S["y_tp"], i + 1)
                dve.wait_ge(out_written, 16 * i + START)
                nc.vector.tensor_tensor(o_sb[:], ps[:, 5, :].rearrange("p (a d) -> p a d", a=CB),
                                        x_sb[:, ds(CB * i, CB), :], ALU.add).then_inc(S["o_ready"], 1)

            for f in range(3):
                gate(0, f)
            keep_lo(0, 0)
            with dve.Fori(0, NCH - 1) as i:
                chunk(i)
            chunk(NCH - 1, last=True)

        @block.tensor
        def _(pe):
            mm, tp = nc.tensor.matmul, nc.tensor.transpose
            pe.sem_inc(S["probs_given_back"], BUFS)
            pe.sem_inc(S["units_done"], BUFS)
            pe.wait_ge(S["silu_c_done"], 1)
            for slot in range(6):
                last = mm(ps[:, 7, slot * B:(slot + 1) * B], wmod_sb[:, slot * D:(slot + 1) * D], silu_c[:],
                          start=True, stop=True)
            last.then_inc(S["mod_mm"], 1)

            pe.wait_ge(S["w_loaded"], 16 * N_WEIGHT_DMAS)
            pe.wait_ge(S["mask_set"], 1)
            pe.wait_ge(S["mod_done"], 1)
            with pe.Fori(0, B) as b:
                pe.wait_ge(S["h_ready"], 2 * b + START)
                for k in range(2):
                    pe.wait_ge(S["xn_ready"], 2 * b + (k + 1))
                    for a in range(CB):
                        last = tp(ps[:, k, a * P:(a + 1) * P], xn[:, k, a, :], identf[:])
                    last.then_inc(S["xt_done"], 1)
                pe.wait_ge(S["v_evac"], 2 * b + START)
                for k in range(2):
                    pe.wait_ge(S["h_ready"], 2 * b + (k + 1) + START)
                    for a in range(CB):
                        last = mm(ps[:, 6 + k, a * P:(a + 1) * P], h_t[:, k, a * P:(a + 1) * P], w_proj[:, 4, :],
                                  start=True, stop=True)
                    last.then_inc(S["v_proj"], 1)
                    pe.wait_ge(S["rope_read"], 4 * b + 2 * k + START)
                    for s in range(2):
                        mm(ps[:, 2 + 2 * s, :], w_proj[:, 2 * s, :], h_t[:, k, :], start=True, stop=True)
                        mm(ps[:, 3 + 2 * s, :], w_proj[:, 2 * s + 1, :], h_t[:, k, :], start=True, stop=True
                           ).then_inc(S["qk_proj"], 1)

            def max_piece(m, v, k, first=False):
                j, pairs, qb, c0, w, part = PIECES[m]
                if not first or m >= 2:
                    pe.wait_ge(S["reduced"], NP * v + (m - 1))
                rows = slice(64 * j, 64 * j + SR + 1)
                for n, p in enumerate(pairs):
                    diagonal = part == 1 or qb < CB
                    last = mm(ps[:, B_MAX + j, n * w:(n + 1) * w], q_s[k][rows, p, qb * P:(qb + 1) * P],
                              k_s[k][rows, p, c0:c0 + w], start=True, stop=True)
                    if diagonal:
                        last = mm(ps[:, B_MAX + j, (n + 1) * w - P:(n + 1) * w], identb[:], maskb[:],
                                  start=False, stop=True, skip_group_check=True)
                last.then_inc(S["pieces_ready"], 1)

            def turn_neg(c, v):
                pe.wait_ge(S["neg_lo"], 2 * v + (c + 1))
                for qb in range(CB):
                    last = tp(ps[0:8, B_MISC, qb * P:(qb + 1) * P],
                              neg_split[:, c, qb].rearrange("p s j h -> p (s j h)").bitcast(F32), identf[:])
                last.then_inc(S["neg_tp"], 1)

            def turn_context(c, u):
                pe.wait_ge(S["ctx_evac"], 2 * u + (c + 1) + START)
                for a in range(CB):
                    last = tp(ps[:, B_MISC, a * P:(a + 1) * P], cat[:, c, a * P:(a + 1) * P], identf[:])
                    if c == 1 and a == 2:
                        last.then_inc(S["units_done"], 1)
                last.then_inc(S["ctx_tp"], 1)

            def weigh_values(q, u, k):
                c, kb, off = KEYS[q]
                if q in DIAGONAL:
                    pe.wait_ge(S["mask_done"], len(DIAGONAL) * u + (DIAGONAL.index(q) + 1))
                else:
                    pe.wait_ge(S["score_banks_free"], STEPS * u + (2 * q + 4))
                if kb == 0:
                    pe.wait_ge(S["v_staged"], u + 1)
                    pe.wait_ge(S["ctx_evac"], 2 * u + c + START)
                for h in range(G):
                    last = mm(ps[32 * h:32 * h + 32, B_CTX, off:], v_unit[:, k, kb, h, :],
                              probs[:, q % BUFS, h, off:], start=kb == 0, stop=kb == CB * (c + 1) - 1)
                last.then_inc(S["probs_given_back"], 1)

            def unit(u, t, k, with_max=True):
                km = (k + 1) % BUFS
                for n in range(STEPS):
                    q, p = divmod(n, 2)
                    c, kb, off = KEYS[q]
                    bank = B_SCORES[n % 2]
                    if n in (0, 2 * CB):
                        pe.wait_ge(neg_loaded[c], 16 * NEG_DMAS * (u + 1) + START)
                    pe.wait_ge(S["score_banks_free"], STEPS * u + (n + 1))
                    for j in range(2):
                        rows = slice(64 * j, 64 * j + ROWS)
                        last = mm(ps[:, bank + j, off:], k_s[k][rows, p, kb * P:(kb + 1) * P],
                                  q_s[k][rows, p, c * CH + off:(c + 1) * CH], start=True, stop=True)
                    last.then_inc(S["scores_ready"], 1)
                    if with_max:
                        if n == 0:
                            pe.wait_ge(qk_loaded[km], 16 * UNIT_DMAS * (t + (1 if km else 2)))
                        for m in range(BEFORE[n - 1] if n else 0, BEFORE[n]):
                            if m == NEG0_AT:
                                pe.wait_ge(S["neg_evac"], 2 * u + 2)
                                turn_neg(0, u + 1)
                            max_piece(m, u + 1, km)
                    if n == 2:
                        pe.wait_ge(S["neg_evac"], 2 * u + 1)
                        pe.wait_ge(S["ctx_finished"], 2 * u + START)
                        turn_neg(1, u)
                    if n % 2 and n >= 3:
                        weigh_values(q - 1, u, k)
                    if n == CTX0_AT:
                        pe.wait_ge(S["neg_evac"], 2 * u + (3 if with_max else 2))
                        turn_context(0, u)
                weigh_values(len(KEYS) - 1, u, k)
                pe.wait_ge(S["ctx_finished"], 2 * u + 1 + START)
                turn_context(1, u)

            pe.wait_ge(qk_loaded[0], 16 * UNIT_DMAS)
            for m in range(NP):
                if m == NEG0_AT:
                    turn_neg(0, 0)
                max_piece(m, 0, 0, first=True)
            with pe.Fori(0, (UNITS - 1) // BUFS) as t:
                for k in range(BUFS):
                    unit(BUFS * t + k, t, k)
            unit(UNITS - 1, (UNITS - 1) // BUFS, 0, with_max=False)

            pe.wait_ge(S["ctx_finished"], 2 * UNITS + START)
            with pe.Fori(0, B) as b:
                pe.wait_ge(S["logit_read"], 2 * b + START)
                for k in range(2):
                    pe.wait_ge(S["ctx_staged"], 2 * b + (k + 1))
                    for a in range(CB):
                        last = tp(ps[:, k, a * P:(a + 1) * P], ctx_st[:, k, a, :], identf[:])
                    last.then_inc(S["ctx2_tp"], 1)
                for k in range(2):
                    pe.wait_ge(S["ctx2_evac"], 2 * b + (k + 1))
                    pe.wait_ge(S["att_evac"], 2 * b + START)
                    mm(ps[:, 2 + k, :], wo_sb[:], ctx_t[:, k, :], start=True, stop=True).then_inc(S["att_mm"], 1)
                for k in range(2):
                    pe.wait_ge(S["att_evac"], 2 * b + (k + 1) + START)
                    pe.wait_ge(S["x2_ready"], 2 * b + START)
                    for a in range(CB):
                        last = tp(ps[:, 4 + k, a * P:(a + 1) * P], att_t[:, k, a * P:(a + 1) * P], identf[:])
                    last.then_inc(S["att_tp"], 1)
                for k in range(2):
                    pe.wait_ge(S["xn_ready"], NCH + 2 * b + (k + 1))
                    pe.wait_ge(S["h_ready"], NCH + 2 * b + START)
                    for a in range(CB):
                        last = tp(ps[:, 6 + k, a * P:(a + 1) * P], xn2[:, k, a, :], identf[:])
                    last.then_inc(S["xt_done"], 1)
                for k in range(2):
                    pe.wait_ge(S["h_ready"], NCH + 2 * b + (k + 1) + START)
                    for a in range(CB):
                        last = mm(ps[:, k, a * E:(a + 1) * E], h2_t[:, k, a * P:(a + 1) * P], wg_sb[:],
                                  start=True, stop=True)
                    last.then_inc(S["logit_mm"], 1)
            pe.wait_ge(S["route_chain"], 12)
            for half in range(2):
                last = tp(ps[:, 5, half * P:(half + 1) * P],
                          sel[:, half * 2 * NB:(half + 1) * 2 * NB, :].rearrange("p n e -> p (n e)"), identf[:])
            last.then_inc(S["ewt_mm"], 1)

            def up(i, f, first=False):
                if not first or f >= 2:
                    pe.wait_ge(S["g_done"], NF * i + (f - 1))
                fs, tok = slice(f * P, (f + 1) * P), ds(i * CH, CH)
                for n, (hi, lo) in enumerate(((w1_hi, w1_lo), (w3_hi, w3_lo))):
                    bank = ps[:, 2 * (f % 2) + n, :]
                    mm(bank, hi[:, fs], h2_hi[:, tok], start=True, stop=False)
                    mm(bank, hi[:, fs], h2_lo[:, tok], start=False, stop=False)
                    last = mm(bank, lo[:, fs], h2_hi[:, tok], start=False, stop=True)
                last.then_inc(S["h_banks"], 1)

            def down(i, f):
                fs = slice(f * P, (f + 1) * P)
                if f == 0:
                    pe.wait_ge(S["y_evac"], i + START)
                pe.wait_ge(S["glo_done"], NF * i + (f + 1))
                mm(ps[:, 4, :], w2_hi[:, fs], g_hi[:, f % 4, :], start=f == 0, stop=False)
                mm(ps[:, 4, :], w2_hi[:, fs], g_lo[:, f % 4, :], start=False, stop=False)
                last = mm(ps[:, 4, :], w2_lo[:, fs], g_hi[:, f % 4, :], start=False, stop=f == NF - 1)
                if f == NF - 1:
                    last.then_inc(S["y_mm"], 1)

            def chunk(i, last_chunk=False):
                for f in range(NF):
                    down(i, f)
                    if f + 3 < NF:
                        up(i, f + 3)
                    elif not last_chunk:
                        up(i + 1, f + 3 - NF)
                pe.wait_ge(S["y_evac"], i + 1 + START)
                pe.wait_ge(S["o_ready"], i + START)
                for a in range(CB):
                    last = tp(ps[:, 5, a * P:(a + 1) * P], y_sb[:, a * P:(a + 1) * P], identf[:])
                last.then_inc(S["y_tp"], 1)

            pe.wait_ge(S["wlo_ready"], B)
            pe.wait_ge(S["h2lo_ready"], NCH + START)
            pe.wait_ge(S["ewt_ready"], 1)
            for f in range(3):
                up(0, f, first=True)
            with pe.Fori(0, NCH - 1) as i:
                chunk(i)
            chunk(NCH - 1, last_chunk=True)


def constants():
    f32 = np.float32
    fraction = (2 * np.arange(HD // 2) / HD).astype(f32)
    timescale = np.power(f32(1250), fraction).astype(f32)
    angle = (np.arange(L).astype(f32)[None, :] / timescale[:, None]).astype(f32)
    sin, cos = np.sin(angle), np.cos(angle)
    rope = np.stack([np.tile(np.concatenate([cos, cos]), (NH, 1)), np.tile(np.concatenate([-sin, sin]), (NH, 1))], 1)
    row, col = np.arange(P)[:, None], np.arange(P)[None, :]
    mask = np.where(col > row, MASKED, 0.0)
    e = np.arange(E)
    before = np.tile((e[None, :] < e[:, None]).astype(f32)[None], (P, 1, 1))
    return {"rope": rope.astype(f32), "ident": np.eye(P, dtype=f32), "mask_up": mask.astype(f32),
            "before": before}


def kernel(**inputs):
    import concourse.bacc as bacc
    from concourse.bass_utils import run_bass_kernel_spmd

    a = {k: np.asarray(v) for k, v in inputs.items()}
    swap = np.arange(D).reshape(NH, 2, HD // 2)[:, ::-1].reshape(D)
    wq, bq, wk, bk = (a[f"L0_attn_w{n}"] for n in ("q_w", "q_b", "k_w", "k_b"))
    arrays = {
        "x": a["L0_attn_x"],
        "w_in5": np.stack([wq, wq[:, swap], wk, wk[:, swap], a["L0_attn_wv_w"]], axis=1),
        "cols_in": np.stack([bq, bq[swap], bk, bk[swap], a["L0_attn_wo_b"]], axis=1),
        "bv": a["L0_attn_wv_b"],
        "wo": a["L0_attn_wo_w"],
        "wgT": a["L0_ffn_wg"].T,
        "w1T": a["L0_ffn_w1"].reshape(E * I, D).T,
        "w3T": a["L0_ffn_w3"].reshape(E * I, D).T,
        "w2T": a["L0_ffn_w2"].reshape(E, D, I // P, P).transpose(3, 0, 2, 1).reshape(P, E * I),
        "cT": a["L0_c"].T,
        "wmod": a["L0_wmod"],
        **constants(),
    }
    nc = bacc.Bacc("TRN2", target_bir_lowering=False, num_devices=1)
    feeds, args = {}, []
    for name, arr in arrays.items():
        arr = np.ascontiguousarray(arr)
        feeds[f"in_{name}"] = arr
        args.append(nc.dram_tensor(f"in_{name}", arr.shape, mybir.dt.from_np(arr.dtype), kind="ExternalInput").ap())
    args.append(nc.dram_tensor("out_0", (B, L, D), F32, kind="ExternalOutput").ap())
    build(nc, *args)
    return run_bass_kernel_spmd(nc, [feeds], core_ids=[0]).results[0]["out_0"]
```

```python
from contextlib import ExitStack

import numpy as np
import concourse.bass as bass
from concourse import mybir

F32 = mybir.dt.float32
F32R = mybir.dt.float32r
BF16 = mybir.dt.bfloat16
ALU = mybir.AluOpType
ACT = mybir.ActivationFunctionType
X = mybir.AxisListType.X
ds = bass.ds

P = 128
B, L, D = 4, 1024, 128
NH, HD = 16, 8
E, I = 8, 256
CH = 512
NCH = B * L // CH
NB = L // P
CB = CH // P
G = 4
UNITS = B * NH // G
NF = E * I // P
HR = P // G
SR = 3 * HD
ROWS = SR + 2
BUFS = 3
MASKED = -3.0e38
EPS = 1e-5
START = 1
SA, CA, GA, SB, CB_, GB = range(6)

RING = 3
B_SCORES, B_CTX, B_MAX, B_MISC = 0, 3, 4, 7


def key_steps():
    out = []
    for c in range(2):
        for kb in range(CB * (c + 1)):
            out.append((c, kb, max(0, kb - CB * c) * P))
    return out


KEYS = key_steps()
NQ = len(KEYS)
SLOTS = NQ * G
LEAD = 2 * G
CTX_EVAC = [G * (q + 2) for q in (CB - 1, NQ - 1)]
ACT_LEAD = CTX_EVAC[1] - SLOTS + 1
DIAGONAL = [q for q, (c, kb, _) in enumerate(KEYS) if kb >= CB * c]


def max_pieces():
    def heads_by(w):
        n = CH // w
        return [range(h, min(h + n, G)) for h in range(0, G, n)]

    out = []
    for qb in range(CB):
        w = (qb + 1) * P
        out += [(hs, qb, 0, w, 0) for hs in heads_by(w)]
    first = len(out)
    for qb in range(CB, NB):
        w = (qb - CB + 1) * P
        out += [(hs, qb, CH, w, 1) for hs in heads_by(w)] + [(hs, qb, 0, CH, 0) for hs in heads_by(CH)]
    return out, first


PIECES, FIRST_CHUNK_PIECES = max_pieces()
NP = len(PIECES)
NEG0_AT = FIRST_CHUNK_PIECES + 4
NEG0_READ_AT = NEG0_AT + 2
LAST_PIECE_BY = SLOTS - 8
NEG1_AT = SLOTS - 6
CTX0_AT = CTX_EVAC[0] - LEAD + 5


def pieces_before():
    time = []
    for n in range(LAST_PIECE_BY):
        score = CH - KEYS[(n + LEAD) % SLOTS // G][2]
        values = 4 * (CH - KEYS[n // G][2]) if n % G == 0 else 0
        time.append(score + values + 500)
    cost = [64 + w * len(heads) for heads, _, _, w, _ in PIECES]
    m, spent, passed, out = 0, 0, 0, []
    for n in range(LAST_PIECE_BY):
        passed += time[n] / sum(time)
        while m < NP and spent < passed * sum(cost):
            spent += cost[m]
            m += 1
        out.append(m)
    return out[:-1] + [NP] * (SLOTS - LAST_PIECE_BY + 1)


BEFORE = pieces_before()


def build(nc, x, w_in5, cols_in, bv, wo, wgT, w1T, w3T, w2T, cT, wmod,
          rope, ident, mask_up, before, out):
    q_dram = nc.dram_tensor("q_split", (UNITS * G, ROWS, L), F32R, kind="Internal").ap()
    k_dram = nc.dram_tensor("k_split", (UNITS * G, SR, L), F32R, kind="Internal").ap()
    ew_dram = nc.dram_tensor("expert_w", (E, B * L), F32, kind="Internal").ap()

    with ExitStack() as ctx:
        def sb(name, shape, dt=F32, where=ctx):
            return where.enter_context(nc.sbuf_tensor(name, shape, dt))

        def sem(name):
            return ctx.enter_context(nc.semaphore(name))

        ps = ctx.enter_context(nc.psum_tensor("ps", [P, 8, CH], F32))

        x_sb = sb("x_sb", [P, B * NB, D])
        wo_sb, identf = sb("wo_sb", [P, D]), sb("identf", [P, P])
        identb = sb("identb", [P, P], BF16)
        maskb = sb("maskb", [P, P], BF16)
        beforej = sb("beforej", [P, E, E])
        wg_sb = sb("wg_sb", [P, E])
        cols = sb("cols", [P, 5])
        c_sb = sb("c_sb", [P, B])
        silu_c = sb("silu_c", [P, B])
        mod = sb("mod", [P, 6, B])
        gate_abs, gate_sign = sb("gate_abs", [P, B]), sb("gate_sign", [P, B])
        mod_now, mod_now2 = sb("mod_now", [P, 6]), sb("mod_now2", [P, 6])
        gb_chunk, gb_now = sb("gb_chunk", [P, B, 2]), sb("gb_now", [P, 1])
        power = sb("power", [P, NB])
        stats, moments = sb("stats", [P, NB, 6]), sb("moments", [P, NB, 2])
        var_eps, rstd = sb("var_eps", [P, NB]), sb("rstd", [P, NB])
        logits = sb("logits", [P, B * NB, E])
        v_all = sb("v_all", [P, UNITS, NB, G * HD])
        ctx_all = sb("ctx_all", [P, UNITS, NB, G * HD])

        def region(*tenants):
            out, sizes = {}, []
            for t in tenants:
                stack = ExitStack()
                sizes.append((sum(int(np.prod(s[1:])) * (2 if d == BF16 else 4) for _, s, d in t), t))
                for name, shape, dt in t:
                    out[name] = sb(name, shape, dt, stack)
                stack.close()
            most = max(s for s, _ in sizes)
            sb(f"region_{len(regions)}", [P, most // 4])
            regions.append(most)
            return out

        regions = []
        k_shape = [P, G, L]
        r1 = region([(f"q{k}", [P, L], F32R) for k in range(BUFS)] + [(f"k{k}", k_shape, F32R) for k in range(2)],
                    [(f"{n}_{h}", [P, E * I], F32R) for n in ("w1", "w3", "w2") for h in ("hi", "lo")])
        q_s = [r1[f"q{k}"] for k in range(BUFS)]
        w1_hi, w1_lo, w3_hi, w3_lo, w2_hi, w2_lo = (r1[f"{n}_{h}"] for n in ("w1", "w3", "w2") for h in ("hi", "lo"))
        r2 = region([("probs", [P, BUFS, G, CH], F32), ("v_unit", [P, BUFS, NB, G, 32], F32)],
                    [("h2_hi", [P, B * L], F32R), ("h2_lo", [P, B * L], F32R),
                     ("y_sb", [P, CH], F32), ("o_sb", [P, CB, D], F32)])
        probs, v_unit, h2_hi, h2_lo, y_sb, o_sb = (
            r2[n] for n in ("probs", "v_unit", "h2_hi", "h2_lo", "y_sb", "o_sb"))
        r3 = region(
            [("rope_sb", [P, 2, L], F32), ("w_proj", [P, 5, D], F32), ("bv_sb", [P, D], F32), ("wmod_sb", [P, 6 * D], F32), ("mask_f", [P, P], F32),
             ("xn", [P, 2, CB, D], F32), ("h_t", [P, 2, CH], F32), ("rot1", [P, 2, CH], F32),
             ("rot2", [P, 2, CH], F32), ("qk_f", [P, 2, 2, CH], F32), ("qk_hi", [P, 2, 2, CH], F32R),
             ("qk_lo", [P, 2, 2, CH], F32R)],
            [("w_in", [P, 3, E * I], F32), ("ctx_st", [P, 2, CB, D], F32), ("ctx_t", [P, 2, CH], F32),
             ("att_t", [P, 2, CH], F32), ("xn2", [P, 2, CB, D], F32), ("h2_t", [P, 2, CH], F32),
             ("rank3", [P, B * NB, E, E], F32)],
            [("below_k2", [P, 3, E * I], F32), ("k2", k_shape, F32R)],
            [("wb", [P, E, CH], F32), ("s_f", [P, 4, CH], F32), ("g_f", [P, 4, CH], F32), ("gw_f", [P, 4, CH], F32),
             ("g_hi", [P, 4, CH], F32R), ("g_lo", [P, 4, CH], F32R)])
        rope_sb, w_proj, bv_sb, wmod_sb, mask_f, xn, h_t, rot1, rot2, qk_f, qk_hi, qk_lo = (
            r3[n] for n in ("rope_sb", "w_proj", "bv_sb", "wmod_sb", "mask_f", "xn", "h_t", "rot1", "rot2", "qk_f", "qk_hi", "qk_lo"))
        k_s = [r1["k0"], r1["k1"], r3["k2"]]
        w_in, ctx_st, ctx_t, att_t, xn2, h2_t, rank3 = (
            r3[n] for n in ("w_in", "ctx_st", "ctx_t", "att_t", "xn2", "h2_t", "rank3"))
        wb, s_f, g_f, gw_f, g_hi, g_lo = (r3[n] for n in ("wb", "s_f", "g_f", "gw_f", "g_hi", "g_lo"))
        neg = sb("neg", [P, 2, G, CB])
        negm = sb("negm", [P, G, CB])
        neg_split = sb("neg_split", [P, 2, CB, G, 2], F32R)
        neg_t = sb("neg_t", [8, 2, CH], F32R)
        cat = sb("cat", [P, 2, CH])
        rsum = sb("rsum", [P, CB, G])
        eqs = sb("eqs", [P, B * NB, E])
        sel, lmax = sb("sel", [P, B * NB, E]), sb("lmax", [P, B * NB])
        ew, ez = sb("ew", [P, B * NB, E]), sb("ez", [P, B * NB])
        ew_t = sb("ew_t", [P, 2, P])

        names = """waited mask_set w_loaded c_loaded x_loaded silu_c_done mod_mm mod_chain mod_done const_set
            ln_stats ln_moments ln_eps rstd_ready mod_cur xn_ready xt_done h_ready v_proj qk_proj rope_read
            qkf_ready hi_ready lo_ready v_evac scratch_written rows_zeroed rows_set zeros_written k2_set
            score_banks_free scores_ready probs_given_back mask_done v_staged units_done pieces_ready
            reduced neg_min neg_hi neg_lo neg_tp neg_evac ctx_evac ctx_tp sums_done ctx_finished
            ctx_staged ctx2_tp ctx2_evac att_mm att_evac att_tp x2_ready logit_mm logit_read h2hi_ready
            h2lo_ready w_in_loaded whi_ready wlo_ready route_chain lmax_sub ex_ready ewt_mm ewt_ready ew_written
            h_banks silu_done g_done gw_done ghi_done glo_done y_mm y_evac y_tp o_ready gb_cur""".split()
        S = {n: sem(n) for n in names}
        qk_loaded = [sem(f"qk_loaded{k}") for k in range(BUFS)]
        neg_loaded = [sem(f"neg_loaded{c}") for c in range(2)]
        wb_loaded = [sem(f"wb_loaded{e}") for e in range(E)]
        out_written = sem("out_written")

        x_v = x.rearrange("b (n p) d -> p b n d", p=P)
        out_v = out.rearrange("b (n p) d -> p (b n) d", p=P)
        block = ctx.enter_context(nc.Block())
        UNIT_DMAS, NEG_DMAS = 8, 4
        N_WEIGHT_DMAS = 9
        SPLIT_DMAS = 2 * 2 * 3

        def wait_alone(eng, semaphore, value):
            eng.wait_ge(semaphore, value)
            eng.sem_inc(S["waited"], 1)

        def norm_stats(dve, n0, done):
            for j in range(NB):
                last = nc.vector.bn_stats(stats[:, j, :], x_sb[:, ds(n0 + j, 1), :].rearrange("p a d -> p (a d)"))
            last.then_inc(S["ln_stats"], 1)
            wait_alone(dve, S["ln_stats"], done)
            for j in range(NB):
                last = nc.vector.bn_aggr(moments[:, j, :], stats[:, j, :])
            last.then_inc(S["ln_moments"], 1)

        def norm_rows(dve, n0, half, dst):
            for a in range(CB):
                j = CB * half + a
                last = nc.vector.tensor_scalar(
                    dst[:, half, a, :], x_sb[:, ds(n0 + j, 1), :].rearrange("p a d -> p (a d)"),
                    moments[:, j, 0:1], rstd[:, j:j + 1], ALU.subtract, ALU.mult)
            last.then_inc(S["xn_ready"], 1)

        def rstd_of(pool, done):
            wait_alone(pool, S["ln_moments"], done)
            nc.gpsimd.tensor_scalar(var_eps[:], moments[:, :, 1], EPS, None, ALU.add).then_inc(S["ln_eps"], 1)
            pool.wait_ge(S["ln_eps"], done)
            nc.gpsimd.tensor_tensor(rstd[:], var_eps[:], power[:], ALU.pow).then_inc(S["rstd_ready"], 1)

        from_start = [S[n] for n in """h_ready xt_done qk_proj qkf_ready lo_ready scratch_written v_evac
            rope_read ctx2_tp att_mm h2lo_ready logit_mm logit_read att_evac att_tp x2_ready ctx_tp
            ctx_finished ctx_evac y_evac o_ready""".split()] + neg_loaded + [out_written]

        @block.sync
        def _(sp):
            for semaphore in from_start:
                sp.sem_inc(semaphore, START)
            with sp.Fori(0, B) as b:
                sp.dma_start(x_sb[:, ds(b * NB, NB), :],
                             x_v[:, ds(b, 1)].rearrange("p a n d -> p (a n) d")).then_inc(S["x_loaded"], 16)
                wait_alone(sp, S["x_loaded"], 16 * b + 16)
            def save_batch(b):
                for k in range(2):
                    cs = slice(k * CH, (k + 1) * CH)
                    for s in range(2):
                        n = 4 * b + (2 * k + s + 1)
                        dst = (q_dram, k_dram)[s][ds(NH * b, NH)]
                        sp.wait_ge(S["hi_ready"], n)
                        for slot in ((0, 1), (0, 2))[s]:
                            sp.dma_start(dst[:, HD * slot:HD * (slot + 1), cs].bitcast(F32), qk_hi[:, s, k, :].bitcast(F32)
                                         ).then_inc(S["scratch_written"], 16)
                        sp.wait_ge(S["lo_ready"], n + START)
                        slot = (2, 1)[s]
                        sp.dma_start(dst[:, HD * slot:HD * (slot + 1), cs].bitcast(F32), qk_lo[:, s, k, :].bitcast(F32)
                                     ).then_inc(S["scratch_written"], 16)
            def load_unit(w, k):
                sp.wait_ge(S["units_done"], w + 1)
                for h in range(G):
                    q_src = q_dram[ds(G * w + h, 1)].rearrange("a r t -> (a r) t")
                    k_src = k_dram[ds(G * w + h, 1)].rearrange("a r t -> (a r) t")
                    sp.dma_start(q_s[k][HR * h:HR * h + ROWS, :].bitcast(F32), q_src.bitcast(F32)
                                 ).then_inc(qk_loaded[k], 16)
                    sp.dma_start(k_s[k][HR * h:HR * h + SR, h, :].bitcast(F32), k_src.bitcast(F32)
                                 ).then_inc(qk_loaded[k], 16)

            def load_neg(u, k, c):
                sp.wait_ge(S["neg_evac"], 2 * u + (c + 1))
                for h in range(G):
                    sp.dma_start(q_s[k][HR * h + SR:HR * h + ROWS, c * CH:(c + 1) * CH].bitcast(F32),
                                 neg_t[2 * h:2 * h + 2, c, :].bitcast(F32)).then_inc(neg_loaded[c], 16)

            save_batch(0)
            sp.wait_ge(S["scratch_written"], 16 * SPLIT_DMAS + START)
            sp.wait_ge(S["zeros_written"], 16)
            sp.wait_ge(S["rows_set"], 1)
            for u in range(2):
                load_unit(u, u)
            with sp.Fori(1, B) as b:
                save_batch(b)
            sp.wait_ge(S["scratch_written"], 16 * SPLIT_DMAS * B + START)
            for n, src in enumerate((w1T, w3T, w2T)):
                sp.dma_start(w_in[:, n, :], src).then_inc(S["w_in_loaded"], 16)
            for c in range(2):
                load_neg(0, 0, c)
            sp.wait_ge(S["k2_set"], 1)
            LOOPED = (UNITS - 2) // BUFS
            with sp.Fori(0, LOOPED) as t:
                for k in range(BUFS):
                    load_unit(BUFS * t + (k + 2), (k + 2) % BUFS)
                    for c in range(2):
                        load_neg(BUFS * t + (k + 1), (k + 1) % BUFS, c)
            for u in range(BUFS * LOOPED, UNITS - 1):
                if u + 2 < UNITS:
                    load_unit(u + 2, (u + 2) % BUFS)
                for c in range(2):
                    load_neg(u + 1, (u + 1) % BUFS, c)

            sp.wait_ge(S["ewt_ready"], 1)
            for half in range(2):
                for n in range(NB * 2):
                    t0 = (half * 2 * NB + n) * P
                    sp.dma_start(ew_dram[:, t0:t0 + P], ew_t[n * E:(n + 1) * E, half, :]).then_inc(S["ew_written"], 16)
            sp.wait_ge(S["ew_written"], 16 * B * NB)
            sp.wait_ge(S["wlo_ready"], B)

            def load_wb(i, e):
                sp.dma_start(wb[:, e, :], ew_dram[e, ds(i * CH, CH)].partition_broadcast(P)).then_inc(wb_loaded[e], 16)

            def store(i):
                sp.wait_ge(S["o_ready"], i + 1 + START)
                sp.dma_start(out_v[:, ds(CB * i, CB), :], o_sb[:]).then_inc(out_written, 16)

            for e in range(E):
                load_wb(0, e)
            with sp.Fori(0, NCH - 1) as i:
                for e in range(E):
                    sp.wait_ge(S["gw_done"], NF * i + (2 * e + 2))
                    load_wb(i + 1, e)
                store(i)
            store(NCH - 1)
            sp.wait_ge(out_written, 16 * NCH + START)

        @block.gpsimd
        def _(pool):
            nc.gpsimd.memset(power[:], -0.5).then_inc(S["const_set"], 1)
            nc.gpsimd.memset(v_unit[:], 0.0).then_inc(S["const_set"], 1)
            pool.wait_ge(S["const_set"], 2)
            nc.gpsimd.memset(v_unit[:, :, :, :, HD:HD + 1], 1.0).then_inc(S["const_set"], 1)
            rstd_of(pool, 1)
            nc.gpsimd.memset(k_s[1][:].bitcast(F32), 0.0)
            for k in range(BUFS):
                last = nc.gpsimd.memset(q_s[k][:].bitcast(F32), 0.0)
            last.then_inc(S["rows_zeroed"], 1)
            pool.wait_ge(S["rows_zeroed"], 2)
            pool.wait_ge(S["zeros_written"], 16)
            for k in range(2):
                for h in range(G):
                    last = nc.gpsimd.memset(k_s[k][HR * h:HR * (h + 1), h, :].bitcast(F32), 1.0)
            last.then_inc(S["rows_set"], 1)
            pool.wait_ge(S["rows_set"], 1)

            def rotate(b, last_batch=False):
                if not last_batch:
                    rstd_of(pool, b + 2)
                for k in range(2):
                    for s in range(2):
                        n = 4 * b + (2 * k + s + 1)
                        pool.wait_ge(S["rope_read"], n + START)
                        pool.wait_ge(S["lo_ready"], 4 * b + START)
                        nc.gpsimd.tensor_tensor(qk_f[:, s, k, :], rot1[:, s, :], rot2[:, s, :], ALU.add
                                                ).then_inc(S["qkf_ready"], 1)

            with pool.Fori(0, B - 1) as b:
                rotate(b)
            rotate(B - 1, last_batch=True)

            def stage_v(w, k):
                pool.wait_ge(S["units_done"], w + 1)
                nc.gpsimd.tensor_copy(
                    v_unit[:, k, :, :, 0:HD],
                    v_all[:, ds(w, 1)].rearrange("p a n (h d) -> p (a n) h d", h=G)).then_inc(S["v_staged"], 1)

            def mask_diagonals(u, c):
                for q in DIAGONAL[CB * c:CB * (c + 1)]:
                    off = KEYS[q][2]
                    wait_alone(pool, S["score_banks_free"], SLOTS * u + (G * (q + 1) + RING))
                    tile = probs[:, q % BUFS, :, off:off + P]
                    nc.gpsimd.affine_select(out=tile, in_=tile, compare_op=ALU.is_ge, fill=0.0, base=0,
                                            pattern=[[0, G], [1, P]], channel_multiplier=-1
                                            ).then_inc(S["mask_done"], 1)

            pool.wait_ge(S["v_evac"], NCH + START)
            pool.wait_ge(S["const_set"], 3)
            stage_v(0, 0)
            with pool.Fori(0, (UNITS - 1) // BUFS) as t:
                for k in range(BUFS):
                    mask_diagonals(BUFS * t + k, 0)
                    stage_v(BUFS * t + (k + 1), (k + 1) % BUFS)
                    mask_diagonals(BUFS * t + k, 1)
            for c in range(2):
                mask_diagonals(UNITS - 1, c)

            pool.wait_ge(S["ctx_finished"], 2 * UNITS + START)
            pool.wait_ge(S["w_in_loaded"], 48)
            with pool.Fori(0, B) as b:
                for k in range(2):
                    pool.wait_ge(S["ctx2_tp"], 2 * b + START)
                    for g in range(NH // G):
                        last = nc.gpsimd.tensor_copy(
                            ctx_st[:, k, :, g * G * HD:(g + 1) * G * HD],
                            ctx_all[:, ds(4 * b + g, 1), CB * k:CB * (k + 1), :].rearrange("p a n d -> p (a n) d"))
                    last.then_inc(S["ctx_staged"], 1)
                rstd_of(pool, B + b + 1)
                for k in range(2):
                    pool.wait_ge(S["h2hi_ready"], 2 * b + (k + 1))
                    nc.gpsimd.tensor_tensor(h2_lo[:, ds((2 * b + k) * CH, CH)], h2_t[:, k, :],
                                            h2_hi[:, ds((2 * b + k) * CH, CH)].bitcast(F32), ALU.subtract
                                            ).then_inc(S["h2lo_ready"], 1)
                pool.wait_ge(S["whi_ready"], b + 1)
                for n, (hi, lo) in enumerate(((w1_hi, w1_lo), (w3_hi, w3_lo), (w2_hi, w2_lo))):
                    last = nc.gpsimd.tensor_tensor(lo[:, ds(b * CH, CH)], w_in[:, n, ds(b * CH, CH)],
                                                   hi[:, ds(b * CH, CH)].bitcast(F32), ALU.subtract)
                last.then_inc(S["wlo_ready"], 1)

            with pool.Fori(0, NCH) as i:
                for f in range(NF):
                    if f % 2 == 0:
                        pool.wait_ge(wb_loaded[f // 2], 16 * i + 16)
                    pool.wait_ge(S["g_done"], NF * i + (f + 1))
                    nc.gpsimd.tensor_tensor(gw_f[:, f % 4, :], g_f[:, f % 4, :], wb[:, f // 2, :], ALU.mult
                                            ).then_inc(S["gw_done"], 1)

        @block.scalar
        def _(act):
            act.dma_start(c_sb[:], cT).then_inc(S["c_loaded"], 16)
            act.dma_start(wmod_sb[:], wmod).then_inc(S["c_loaded"], 16)
            for dst, src in ((w_proj[:], w_in5), (cols[:], cols_in), (identf[:], ident), (mask_f[:], mask_up),
                             (rope_sb[:], rope), (wo_sb[:], wo), (wg_sb[:], wgT),
                             (bv_sb[:], bv.partition_broadcast(P))):
                act.dma_start(dst, src).then_inc(S["w_loaded"], 16)
            act.dma_start(beforej[:], before).then_inc(S["w_loaded"], 16)
            act.wait_ge(S["rows_zeroed"], 1)
            act.dma_start(q_dram[:, SR:ROWS, :].bitcast(F32),
                          k_s[0][0:UNITS * G, 0:2, :].bitcast(F32)).then_inc(S["zeros_written"], 16)
            act.sem_inc(S["score_banks_free"], RING)
            act.wait_ge(S["c_loaded"], 32)
            nc.scalar.activation(silu_c[:], c_sb[:], ACT.Silu).then_inc(S["silu_c_done"], 1)

            act.wait_ge(S["mod_done"], 1)
            with act.Fori(0, B) as b:
                act.wait_ge(S["mod_cur"], b + 1)
                for k in range(2):
                    act.wait_ge(S["xt_done"], 2 * b + (k + 1) + START)
                    act.wait_ge(S["qk_proj"], 4 * b + START)
                    nc.scalar.activation(h_t[:, k, :], ps[:, k, :], ACT.Identity, bias=mod_now[:, SA:SA + 1],
                                         scale=mod_now[:, CA:CA + 1]).then_inc(S["h_ready"], 1)
                for k in range(2):
                    for s in range(2):
                        act.wait_ge(S["qkf_ready"], 4 * b + (2 * k + s + 1) + START)
                        act.wait_ge(S["scratch_written"], 16 * SPLIT_DMAS * b + START)
                        nc.scalar.activation(qk_hi[:, s, k, :], qk_f[:, s, k, :], ACT.Copy
                                             ).then_inc(S["hi_ready"], 1)

            def exp(u, n):
                q, h = divmod(n, G)
                off = KEYS[q][2]
                act.wait_ge(S["scores_ready"], SLOTS * u + (n + 1))
                if h == 0:
                    act.wait_ge(S["probs_given_back"], NQ * u + (q + 1))
                nc.scalar.activation(probs[:, q % BUFS, h, off:], ps[:, B_SCORES + n % RING, off:],
                                     ACT.Exp, scale=float(HD) ** -0.5).then_inc(S["score_banks_free"], 1)

            def evacuate_context(u, c):
                act.wait_ge(S["probs_given_back"], NQ * u + (BUFS + (CB, NQ)[c]))
                act.wait_ge(S["ctx_tp"], 2 * u + START)
                nc.scalar.activation(cat[:, c, :], ps[:, B_CTX, :], ACT.Copy).then_inc(S["ctx_evac"], 1)

            def unit(u, last=False):
                for n in range(ACT_LEAD, SLOTS + ACT_LEAD):
                    if n < SLOTS:
                        exp(u, n)
                    elif not last:
                        exp(u + 1, n - SLOTS)
                    if n in CTX_EVAC:
                        evacuate_context(u, CTX_EVAC.index(n))

            for n in range(ACT_LEAD):
                exp(0, n)
            with act.Fori(0, (UNITS - 1) // BUFS) as t:
                for k in range(BUFS):
                    unit(BUFS * t + k)
            unit(UNITS - 1, last=True)

            act.wait_ge(S["w_in_loaded"], 48)
            act.wait_ge(S["ctx_finished"], 2 * UNITS + START)
            with act.Fori(0, B) as b:
                for k in range(2):
                    act.wait_ge(S["ctx2_tp"], 2 * b + (k + 1) + START)
                    act.wait_ge(S["att_mm"], 2 * b + START)
                    nc.scalar.activation(ctx_t[:, k, :], ps[:, k, :], ACT.Copy).then_inc(S["ctx2_evac"], 1)
                for n, hi in enumerate((w1_hi, w3_hi, w2_hi)):
                    last = nc.scalar.activation(hi[:, ds(b * CH, CH)], w_in[:, n, ds(b * CH, CH)], ACT.Copy)
                last.then_inc(S["whi_ready"], 1)
                act.wait_ge(S["mod_cur"], B + b + 1)
                for k in range(2):
                    act.wait_ge(S["xt_done"], NCH + 2 * b + (k + 1) + START)
                    act.wait_ge(S["h2lo_ready"], 2 * b + START)
                    act.wait_ge(S["logit_mm"], 2 * b + START)
                    nc.scalar.activation(h2_t[:, k, :], ps[:, 6 + k, :], ACT.Identity, bias=mod_now2[:, SB:SB + 1],
                                         scale=mod_now2[:, CB_:CB_ + 1]).then_inc(S["h_ready"], 1)
                for k in range(2):
                    act.wait_ge(S["h_ready"], NCH + 2 * b + (k + 1) + START)
                    nc.scalar.activation(h2_hi[:, ds((2 * b + k) * CH, CH)], h2_t[:, k, :], ACT.Copy
                                         ).then_inc(S["h2hi_ready"], 1)
            act.wait_ge(S["lmax_sub"], 1)
            nc.scalar.activation(ew[:], ew[:], ACT.Exp).then_inc(S["ex_ready"], 1)

            def silu(i, f):
                act.wait_ge(S["h_banks"], NF * i + (f + 1))
                nc.scalar.activation(s_f[:, f % 4, :], ps[:, 2 * (f % 2), :], ACT.Silu).then_inc(S["silu_done"], 1)

            def keep_hi(i, f):
                act.wait_ge(S["gw_done"], NF * i + (f + 1))
                nc.scalar.activation(g_hi[:, f % 4, :], gw_f[:, f % 4, :], ACT.Copy).then_inc(S["ghi_done"], 1)

            def chunk(i, last=False):
                for f in range(NF):
                    if f + 1 < NF:
                        keep_hi(i, f + 1)
                    elif not last:
                        keep_hi(i + 1, 0)
                    if f + 3 < NF:
                        silu(i, f + 3)
                    elif not last:
                        silu(i + 1, f + 3 - NF)

            for f in range(3):
                silu(0, f)
            keep_hi(0, 0)
            with act.Fori(0, NCH - 1) as i:
                chunk(i)
            chunk(NCH - 1, last=True)

        @block.vector
        def _(dve):
            nc.vector.memset(k_s[0][:].bitcast(F32), 0.0).then_inc(S["rows_zeroed"], 1)
            dve.wait_ge(S["x_loaded"], 16)
            norm_stats(dve, 0, 1)
            dve.wait_ge(S["mod_mm"], 1)
            nc.vector.tensor_copy(mod[:].rearrange("p s b -> p (s b)"), ps[:, 7, 0:6 * B]).then_inc(S["mod_chain"], 1)
            dve.wait_ge(S["mod_chain"], 1)
            for slot in (CA, CB_):
                nc.vector.tensor_scalar(mod[:, slot, :], mod[:, slot, :], 1.0, None, ALU.add)
            n = 1
            for slot in (GA, GB):
                nc.vector.tensor_scalar(gate_sign[:], mod[:, slot, :], 0.0, 2.0, ALU.is_ge, ALU.mult)
                nc.vector.scalar_tensor_tensor(gate_abs[:], mod[:, slot, :], -1.0, mod[:, slot, :], ALU.mult, ALU.max
                                               ).then_inc(S["mod_chain"], 1)
                n += 1
                dve.wait_ge(S["mod_chain"], n)
                nc.vector.tensor_scalar(gate_abs[:], gate_abs[:], 0.25, None, ALU.max).then_inc(S["mod_chain"], 1)
                n += 1
                dve.wait_ge(S["mod_chain"], n)
                nc.vector.scalar_tensor_tensor(mod[:, slot, :], gate_sign[:], -1.0, gate_abs[:], ALU.add, ALU.mult
                                               ).then_inc(S["mod_chain"], 1)
                n += 1
                dve.wait_ge(S["mod_chain"], n)
            for k in range(2):
                last = nc.vector.tensor_copy(gb_chunk[:, :, k], mod[:, GB, :])
            last.then_inc(S["mod_done"], 1)
            dve.wait_ge(S["mod_done"], 1)

            dve.wait_ge(S["w_loaded"], 16 * N_WEIGHT_DMAS)
            nc.vector.tensor_copy(identb[:], identf[:])
            nc.vector.tensor_copy(maskb[:], mask_f[:]).then_inc(S["mask_set"], 1)
            def keep_lo_of(b):
                for k in range(2):
                    for s in range(2):
                        dve.wait_ge(S["hi_ready"], 4 * b + (2 * k + s + 1))
                        dve.wait_ge(S["scratch_written"], 16 * SPLIT_DMAS * b + START)
                        nc.vector.tensor_tensor(qk_lo[:, s, k, :], qk_f[:, s, k, :], qk_hi[:, s, k, :].bitcast(F32),
                                                ALU.subtract).then_inc(S["lo_ready"], 1)

            def batch(b, first=False, last_batch=False):
                dve.wait_ge(S["h_ready"], 2 * b + START)
                nc.vector.tensor_copy(mod_now[:], mod[:, :, ds(b, 1)].rearrange("p s a -> p (s a)")
                                      ).then_inc(S["mod_cur"], 1)
                dve.wait_ge(S["rstd_ready"], b + 1)
                dve.wait_ge(S["xt_done"], 2 * b + START)
                for k in range(2):
                    norm_rows(dve, NB * b, k, xn)
                if not first:
                    keep_lo_of(b - 1)
                if not last_batch:
                    dve.wait_ge(S["xn_ready"], 2 * b + 2)
                    wait_alone(dve, S["x_loaded"], 16 * (b + 1) + 16)
                    norm_stats(dve, NB * (b + 1), b + 2)
                for k in range(2):
                    cs = slice(k * CH, (k + 1) * CH)
                    dve.wait_ge(S["v_proj"], 2 * b + (k + 1))
                    for a in range(CB):
                        last = nc.vector.tensor_tensor(
                            v_all[:, ds(4 * b, 4), CB * k + a, :],
                            ps[:, 6 + k, a * P:(a + 1) * P].rearrange("p (g d) -> p g d", g=4),
                            bv_sb[:].rearrange("p (g d) -> p g d", g=4), ALU.add)
                    last.then_inc(S["v_evac"], 1)
                    for s in range(2):
                        dve.wait_ge(S["qk_proj"], 4 * b + (2 * k + s + 1) + START)
                        dve.wait_ge(S["qkf_ready"], 4 * b + (k * (s + 1)) + START)
                        nc.vector.scalar_tensor_tensor(rot1[:, s, :], ps[:, 2 + 2 * s, :], cols[:, 2 * s:2 * s + 1],
                                                       rope_sb[:, 0, cs], ALU.add, ALU.mult)
                        nc.vector.scalar_tensor_tensor(rot2[:, s, :], ps[:, 3 + 2 * s, :],
                                                       cols[:, 2 * s + 1:2 * s + 2], rope_sb[:, 1, cs], ALU.add,
                                                       ALU.mult).then_inc(S["rope_read"], 1)

            batch(0, first=True)
            with dve.Fori(1, B - 1) as b:
                batch(b)
            batch(B - 1, last_batch=True)
            keep_lo_of(B - 1)

            def reduce_piece(m, v, k):
                heads, qb, _, w, part = PIECES[m]
                n = len(heads)
                dve.wait_ge(S["pieces_ready"], NP * v + (m + 1))
                nc.vector.tensor_reduce(neg[:, part, heads[0]:heads[-1] + 1, qb % CB],
                                        ps[:, B_MAX + (NP * k + m) % RING, 0:n * w].rearrange("p (n w) -> p n w", n=n),
                                        axis=X, op=ALU.max, negate=True).then_inc(S["reduced"], 1)

            def split_neg(c, v):
                dst = neg_split[:, c].rearrange("p q h s -> p h q s")
                src = neg[:, 0]
                dve.wait_ge(S["reduced"], NP * v + (NP if c else FIRST_CHUNK_PIECES))
                if c:
                    nc.vector.tensor_tensor(negm[:], neg[:, 0], neg[:, 1], ALU.min).then_inc(S["neg_min"], 1)
                    dve.wait_ge(S["neg_min"], v + 1)
                    src = negm[:]
                nc.vector.tensor_copy(dst[:, :, :, 0], src).then_inc(S["neg_hi"], 1)
                dve.wait_ge(S["neg_hi"], 2 * v + (c + 1))
                nc.vector.tensor_tensor(dst[:, :, :, 1], src, dst[:, :, :, 0].bitcast(F32), ALU.subtract
                                        ).then_inc(S["neg_lo"], 1)

            def read_neg(c, v):
                dve.wait_ge(S["neg_tp"], 2 * v + (c + 1))
                dve.wait_ge(neg_loaded[c], 16 * NEG_DMAS * v + START)
                nc.vector.tensor_copy(neg_t[:, c, :], ps[0:8, B_MISC, :]).then_inc(S["neg_evac"], 1)

            def finish_context(c, u):
                heads = ps[:, B_MISC, :].rearrange("p (a h r) -> p a h r", a=CB, h=G)
                dve.wait_ge(S["ctx_tp"], 2 * u + (c + 1) + START)
                nc.vector.reciprocal(rsum[:], heads[:, :, :, HD]).then_inc(S["sums_done"], 1)
                dve.wait_ge(S["sums_done"], 2 * u + (c + 1))
                nc.vector.tensor_tensor(
                    ctx_all[:, ds(u, 1), CB * c:CB * (c + 1), :].rearrange("p a n (h d) -> p (a n) h d", h=G),
                    heads[:, :, :, 0:HD], rsum[:].unsqueeze(3).broadcast_to([P, CB, G, HD]), ALU.mult
                ).then_inc(S["ctx_finished"], 1)

            def maxima(v, k, m):
                if m == FIRST_CHUNK_PIECES:
                    split_neg(0, v)
                if m == FIRST_CHUNK_PIECES + 1:
                    dve.wait_ge(S["neg_lo"], 2 * v + 1)
                if m == NEG0_READ_AT:
                    read_neg(0, v)
                reduce_piece(m, v, k)
                if m == NP - 1:
                    split_neg(1, v)

            def unit(u, k, last=False):
                for n in range(SLOTS):
                    if not last:
                        for m in range(BEFORE[n - 1] if n else 0, BEFORE[n]):
                            maxima(u + 1, (k + 1) % BUFS, m)
                        if n == NEG1_AT + 1:
                            read_neg(1, u + 1)
                    if n == CTX0_AT + 1:
                        finish_context(0, u)
                finish_context(1, u)

            for m in range(NP):
                maxima(0, 0, m)
            read_neg(1, 0)
            dve.wait_ge(S["scratch_written"], 16 * SPLIT_DMAS * B + START)
            nc.vector.memset(k_s[2][:].bitcast(F32), 0.0).then_inc(S["rows_zeroed"], 1)
            dve.wait_ge(S["rows_zeroed"], 3)
            for h in range(G):
                last = nc.vector.memset(k_s[2][HR * h:HR * (h + 1), h, :].bitcast(F32), 1.0)
            last.then_inc(S["k2_set"], 1)
            with dve.Fori(0, (UNITS - 1) // BUFS) as t:
                for k in range(BUFS):
                    unit(BUFS * t + k, k)
            unit(UNITS - 1, 0, last=True)

            with dve.Fori(0, B) as b:
                dve.wait_ge(S["h_ready"], NCH + 2 * b + START)
                nc.vector.tensor_copy(mod_now2[:], mod[:, :, ds(b, 1)].rearrange("p s a -> p (s a)")
                                      ).then_inc(S["mod_cur"], 1)
                dve.wait_ge(S["mod_cur"], B + b + 1)
                for k in range(2):
                    dve.wait_ge(S["att_mm"], 2 * b + (k + 1) + START)
                    dve.wait_ge(S["att_tp"], 2 * b + START)
                    nc.vector.tensor_scalar(att_t[:, k, :], ps[:, 2 + k, :], cols[:, 4:5], mod_now2[:, GA:GA + 1],
                                            ALU.add, ALU.mult).then_inc(S["att_evac"], 1)
                for k in range(2):
                    rows = x_sb[:, ds(NB * b + CB * k, CB), :]
                    dve.wait_ge(S["att_tp"], 2 * b + (k + 1) + START)
                    nc.vector.tensor_tensor(rows, ps[:, 4 + k, :].rearrange("p (a d) -> p a d", a=CB), rows, ALU.add
                                            ).then_inc(S["x2_ready"], 1)
                wait_alone(dve, S["x2_ready"], 2 * b + 2 + START)
                norm_stats(dve, NB * b, B + b + 1)
                dve.wait_ge(S["rstd_ready"], B + b + 1)
                dve.wait_ge(S["xt_done"], NCH + 2 * b + START)
                for k in range(2):
                    norm_rows(dve, NB * b, k, xn2)
                for k in range(2):
                    dve.wait_ge(S["logit_mm"], 2 * b + (k + 1) + START)
                    nc.vector.tensor_copy(logits[:, ds(NB * b + CB * k, CB), :],
                                          ps[:, k, 0:CB * E].rearrange("p (a e) -> p a e", a=CB)
                                          ).then_inc(S["logit_read"], 1)

            step = [0]

            def chained(ins):
                step[0] += 1
                ins.then_inc(S["route_chain"], 1)
                dve.wait_ge(S["route_chain"], step[0])

            T = B * NB
            dve.wait_ge(S["logit_read"], NCH + START)
            by_e = logits[:].unsqueeze(3).broadcast_to([P, T, E, E])
            by_j = logits[:].unsqueeze(2).broadcast_to([P, T, E, E])
            chained(nc.vector.reduce_max(lmax[:], logits[:], axis=X))
            nc.vector.tensor_tensor(ew[:], logits[:], lmax[:].unsqueeze(2).broadcast_to([P, T, E]), ALU.subtract
                                    ).then_inc(S["lmax_sub"], 1)
            chained(nc.vector.tensor_tensor(rank3[:], by_j, by_e, ALU.is_equal))
            chained(nc.vector.tensor_tensor(rank3[:], rank3[:], beforej[:].unsqueeze(1).broadcast_to([P, T, E, E]),
                                            ALU.mult))
            chained(nc.vector.reduce_sum(eqs[:], rank3[:], axis=X))
            chained(nc.vector.tensor_tensor(rank3[:], by_j, by_e, ALU.is_gt))
            chained(nc.vector.reduce_sum(sel[:], rank3[:], axis=X))
            chained(nc.vector.tensor_tensor(sel[:], sel[:], eqs[:], ALU.add))
            chained(nc.vector.tensor_scalar(sel[:], sel[:], 1.5, None, ALU.is_lt))
            dve.wait_ge(S["ex_ready"], 1)
            chained(nc.vector.tensor_tensor(ew[:], ew[:], sel[:], ALU.mult))
            chained(nc.vector.reduce_sum(ez[:], ew[:], axis=X))
            chained(nc.vector.reciprocal(ez[:], ez[:]))
            nc.vector.tensor_tensor(sel[:], ew[:], ez[:].unsqueeze(2).broadcast_to([P, T, E]), ALU.mult
                                    ).then_inc(S["route_chain"], 1)
            dve.wait_ge(S["ewt_mm"], 1)
            nc.vector.tensor_copy(ew_t[:], ps[:, 5, 0:2 * P].rearrange("p (h t) -> p h t", h=2)
                                  ).then_inc(S["ewt_ready"], 1)

            def gate(i, f):
                dve.wait_ge(S["silu_done"], NF * i + (f + 1))
                nc.vector.tensor_tensor(g_f[:, f % 4, :], ps[:, 2 * (f % 2) + 1, :], s_f[:, f % 4, :], ALU.mult
                                        ).then_inc(S["g_done"], 1)

            def keep_lo(i, f):
                dve.wait_ge(S["ghi_done"], NF * i + (f + 1))
                nc.vector.tensor_tensor(g_lo[:, f % 4, :], gw_f[:, f % 4, :], g_hi[:, f % 4, :].bitcast(F32),
                                        ALU.subtract).then_inc(S["glo_done"], 1)

            def chunk(i, last=False):
                nc.vector.tensor_copy(gb_now[:], gb_chunk[:].rearrange("p b k -> p (b k)")[:, ds(i, 1)]
                                      ).then_inc(S["gb_cur"], 1)
                for f in range(NF):
                    if f + 1 < NF:
                        keep_lo(i, f + 1)
                    elif not last:
                        keep_lo(i + 1, 0)
                    if f == NF - 1:
                        dve.wait_ge(S["gb_cur"], i + 1)
                        dve.wait_ge(S["y_mm"], i + 1)
                        nc.vector.tensor_scalar(y_sb[:], ps[:, 4, :], gb_now[:, 0:1], None, ALU.mult
                                                ).then_inc(S["y_evac"], 1)
                    if f + 3 < NF:
                        gate(i, f + 3)
                    elif not last:
                        gate(i + 1, f + 3 - NF)
                dve.wait_ge(S["y_tp"], i + 1)
                dve.wait_ge(out_written, 16 * i + START)
                nc.vector.tensor_tensor(o_sb[:], ps[:, 5, :].rearrange("p (a d) -> p a d", a=CB),
                                        x_sb[:, ds(CB * i, CB), :], ALU.add).then_inc(S["o_ready"], 1)

            for f in range(3):
                gate(0, f)
            keep_lo(0, 0)
            with dve.Fori(0, NCH - 1) as i:
                chunk(i)
            chunk(NCH - 1, last=True)

        @block.tensor
        def _(pe):
            mm, tp = nc.tensor.matmul, nc.tensor.transpose
            pe.sem_inc(S["probs_given_back"], BUFS)
            pe.sem_inc(S["units_done"], BUFS)
            pe.wait_ge(S["silu_c_done"], 1)
            for slot in range(6):
                last = mm(ps[:, 7, slot * B:(slot + 1) * B], wmod_sb[:, slot * D:(slot + 1) * D], silu_c[:],
                          start=True, stop=True)
            last.then_inc(S["mod_mm"], 1)

            pe.wait_ge(S["w_loaded"], 16 * N_WEIGHT_DMAS)
            pe.wait_ge(S["mask_set"], 1)
            pe.wait_ge(S["mod_done"], 1)
            with pe.Fori(0, B) as b:
                pe.wait_ge(S["h_ready"], 2 * b + START)
                for k in range(2):
                    pe.wait_ge(S["xn_ready"], 2 * b + (k + 1))
                    for a in range(CB):
                        last = tp(ps[:, k, a * P:(a + 1) * P], xn[:, k, a, :], identf[:])
                    last.then_inc(S["xt_done"], 1)
                pe.wait_ge(S["v_evac"], 2 * b + START)
                for k in range(2):
                    pe.wait_ge(S["h_ready"], 2 * b + (k + 1) + START)
                    for a in range(CB):
                        last = mm(ps[:, 6 + k, a * P:(a + 1) * P], h_t[:, k, a * P:(a + 1) * P], w_proj[:, 4, :],
                                  start=True, stop=True)
                    last.then_inc(S["v_proj"], 1)
                    pe.wait_ge(S["rope_read"], 4 * b + 2 * k + START)
                    for s in range(2):
                        mm(ps[:, 2 + 2 * s, :], w_proj[:, 2 * s, :], h_t[:, k, :], start=True, stop=True)
                        mm(ps[:, 3 + 2 * s, :], w_proj[:, 2 * s + 1, :], h_t[:, k, :], start=True, stop=True
                           ).then_inc(S["qk_proj"], 1)

            def max_piece(m, v, k, first=False):
                heads, qb, c0, w, part = PIECES[m]
                if not first or m >= RING:
                    pe.wait_ge(S["reduced"], NP * v + (m - RING + 1))
                bank = B_MAX + (NP * k + m) % RING
                for n, h in enumerate(heads):
                    last = mm(ps[:, bank, n * w:(n + 1) * w], q_s[k][:, qb * P:(qb + 1) * P],
                              k_s[k][:, h, c0:c0 + w], start=True, stop=True)
                    if part == 1 or qb < CB:
                        last = mm(ps[:, bank, (n + 1) * w - P:(n + 1) * w], identb[:], maskb[:],
                                  start=False, stop=True, skip_group_check=True)
                last.then_inc(S["pieces_ready"], 1)

            def turn_neg(c, v):
                pe.wait_ge(S["neg_lo"], 2 * v + (c + 1))
                for qb in range(CB):
                    last = tp(ps[0:8, B_MISC, qb * P:(qb + 1) * P],
                              neg_split[:, c, qb].rearrange("p h s -> p (h s)").bitcast(F32), identf[:])
                last.then_inc(S["neg_tp"], 1)

            def turn_context(c, u):
                pe.wait_ge(S["ctx_evac"], 2 * u + (c + 1) + START)
                for a in range(CB):
                    last = tp(ps[:, B_MISC, a * P:(a + 1) * P], cat[:, c, a * P:(a + 1) * P], identf[:])
                last.then_inc(S["ctx_tp"], 1)

            def weigh_values(q, u, k):
                c, kb, off = KEYS[q]
                if q in DIAGONAL:
                    pe.wait_ge(S["mask_done"], len(DIAGONAL) * u + (DIAGONAL.index(q) + 1))
                else:
                    pe.wait_ge(S["score_banks_free"], SLOTS * u + (G * (q + 1) + RING))
                if kb == 0:
                    pe.wait_ge(S["v_staged"], u + 1)
                    pe.wait_ge(S["ctx_evac"], 2 * u + c + START)
                for h in range(G):
                    last = mm(ps[32 * h:32 * h + 32, B_CTX, off:], v_unit[:, k, kb, h, :],
                              probs[:, q % BUFS, h, off:], start=kb == 0, stop=kb == CB * (c + 1) - 1)
                    if q == NQ - 1 and h == G - 2:
                        last.then_inc(S["units_done"], 1)
                last.then_inc(S["probs_given_back"], 1)

            def score(u, k, n):
                q, h = divmod(n, G)
                c, kb, off = KEYS[q]
                if kb == h == 0:
                    pe.wait_ge(neg_loaded[c], 16 * NEG_DMAS * (u + 1) + START)
                pe.wait_ge(S["score_banks_free"], SLOTS * u + (n + 1))
                mm(ps[:, B_SCORES + n % RING, off:], k_s[k][:, h, kb * P:(kb + 1) * P],
                   q_s[k][:, c * CH + off:(c + 1) * CH], start=True, stop=True).then_inc(S["scores_ready"], 1)

            def unit(u, t, k, last=False):
                km = (k + 1) % BUFS
                if not last:
                    pe.wait_ge(qk_loaded[km], 16 * UNIT_DMAS * (t + (1 if km else 2)))
                for n in range(SLOTS):
                    if n + LEAD < SLOTS:
                        score(u, k, n + LEAD)
                    elif not last:
                        score(u + 1, km, n + LEAD - SLOTS)
                    if not last:
                        for m in range(BEFORE[n - 1] if n else 0, BEFORE[n]):
                            if m == NEG0_AT:
                                pe.wait_ge(S["ctx_finished"], 2 * u + START)
                                turn_neg(0, u + 1)
                            max_piece(m, u + 1, km)
                        if n == NEG1_AT:
                            pe.wait_ge(S["ctx_finished"], 2 * u + 1 + START)
                            turn_neg(1, u + 1)
                    if n % G == 0:
                        weigh_values(n // G, u, k)
                    if n in (CTX0_AT, SLOTS - 1):
                        c = int(n == SLOTS - 1)
                        if last:
                            pe.wait_ge(S["ctx_finished"], 2 * u + c + START)
                        else:
                            pe.wait_ge(S["neg_evac"], 2 * u + (3 + c))
                        turn_context(c, u)

            pe.wait_ge(S["v_evac"], NCH + START)
            pe.wait_ge(S["rope_read"], 4 * B + START)
            pe.wait_ge(qk_loaded[0], 16 * UNIT_DMAS)
            for m in range(NP):
                if m == NEG0_AT:
                    turn_neg(0, 0)
                max_piece(m, 0, 0, first=True)
            pe.wait_ge(S["neg_evac"], 1)
            turn_neg(1, 0)
            for n in range(LEAD):
                score(0, 0, n)
            with pe.Fori(0, (UNITS - 1) // BUFS) as t:
                for k in range(BUFS):
                    unit(BUFS * t + k, t, k)
            unit(UNITS - 1, (UNITS - 1) // BUFS, 0, last=True)

            pe.wait_ge(S["ctx_finished"], 2 * UNITS + START)
            with pe.Fori(0, B) as b:
                pe.wait_ge(S["logit_read"], 2 * b + START)
                for k in range(2):
                    pe.wait_ge(S["ctx_staged"], 2 * b + (k + 1))
                    for a in range(CB):
                        last = tp(ps[:, k, a * P:(a + 1) * P], ctx_st[:, k, a, :], identf[:])
                    last.then_inc(S["ctx2_tp"], 1)
                for k in range(2):
                    pe.wait_ge(S["ctx2_evac"], 2 * b + (k + 1))
                    pe.wait_ge(S["att_evac"], 2 * b + START)
                    mm(ps[:, 2 + k, :], wo_sb[:], ctx_t[:, k, :], start=True, stop=True).then_inc(S["att_mm"], 1)
                for k in range(2):
                    pe.wait_ge(S["att_evac"], 2 * b + (k + 1) + START)
                    pe.wait_ge(S["x2_ready"], 2 * b + START)
                    for a in range(CB):
                        last = tp(ps[:, 4 + k, a * P:(a + 1) * P], att_t[:, k, a * P:(a + 1) * P], identf[:])
                    last.then_inc(S["att_tp"], 1)
                for k in range(2):
                    pe.wait_ge(S["xn_ready"], NCH + 2 * b + (k + 1))
                    pe.wait_ge(S["h_ready"], NCH + 2 * b + START)
                    for a in range(CB):
                        last = tp(ps[:, 6 + k, a * P:(a + 1) * P], xn2[:, k, a, :], identf[:])
                    last.then_inc(S["xt_done"], 1)
                for k in range(2):
                    pe.wait_ge(S["h_ready"], NCH + 2 * b + (k + 1) + START)
                    for a in range(CB):
                        last = mm(ps[:, k, a * E:(a + 1) * E], h2_t[:, k, a * P:(a + 1) * P], wg_sb[:],
                                  start=True, stop=True)
                    last.then_inc(S["logit_mm"], 1)
            pe.wait_ge(S["route_chain"], 12)
            for half in range(2):
                last = tp(ps[:, 5, half * P:(half + 1) * P],
                          sel[:, half * 2 * NB:(half + 1) * 2 * NB, :].rearrange("p n e -> p (n e)"), identf[:])
            last.then_inc(S["ewt_mm"], 1)

            def up(i, f, first=False):
                if not first or f >= 2:
                    pe.wait_ge(S["g_done"], NF * i + (f - 1))
                fs, tok = slice(f * P, (f + 1) * P), ds(i * CH, CH)
                for n, (hi, lo) in enumerate(((w1_hi, w1_lo), (w3_hi, w3_lo))):
                    bank = ps[:, 2 * (f % 2) + n, :]
                    mm(bank, hi[:, fs], h2_hi[:, tok], start=True, stop=False)
                    mm(bank, hi[:, fs], h2_lo[:, tok], start=False, stop=False)
                    last = mm(bank, lo[:, fs], h2_hi[:, tok], start=False, stop=True)
                last.then_inc(S["h_banks"], 1)

            def down(i, f):
                fs = slice(f * P, (f + 1) * P)
                if f == 0:
                    pe.wait_ge(S["y_evac"], i + START)
                pe.wait_ge(S["glo_done"], NF * i + (f + 1))
                mm(ps[:, 4, :], w2_hi[:, fs], g_hi[:, f % 4, :], start=f == 0, stop=False)
                mm(ps[:, 4, :], w2_hi[:, fs], g_lo[:, f % 4, :], start=False, stop=False)
                last = mm(ps[:, 4, :], w2_lo[:, fs], g_hi[:, f % 4, :], start=False, stop=f == NF - 1)
                if f == NF - 1:
                    last.then_inc(S["y_mm"], 1)

            def chunk(i, last_chunk=False):
                for f in range(NF):
                    down(i, f)
                    if f + 3 < NF:
                        up(i, f + 3)
                    elif not last_chunk:
                        up(i + 1, f + 3 - NF)
                pe.wait_ge(S["y_evac"], i + 1 + START)
                pe.wait_ge(S["o_ready"], i + START)
                for a in range(CB):
                    last = tp(ps[:, 5, a * P:(a + 1) * P], y_sb[:, a * P:(a + 1) * P], identf[:])
                last.then_inc(S["y_tp"], 1)

            pe.wait_ge(S["wlo_ready"], B)
            pe.wait_ge(S["h2lo_ready"], NCH + START)
            pe.wait_ge(S["ewt_ready"], 1)
            for f in range(3):
                up(0, f, first=True)
            with pe.Fori(0, NCH - 1) as i:
                chunk(i)
            chunk(NCH - 1, last_chunk=True)


def constants():
    f32 = np.float32
    fraction = (2 * np.arange(HD // 2) / HD).astype(f32)
    timescale = np.power(f32(1250), fraction).astype(f32)
    angle = (np.arange(L).astype(f32)[None, :] / timescale[:, None]).astype(f32)
    sin, cos = np.sin(angle), np.cos(angle)
    rope = np.stack([np.tile(np.concatenate([cos, cos]), (NH, 1)), np.tile(np.concatenate([-sin, sin]), (NH, 1))], 1)
    row, col = np.arange(P)[:, None], np.arange(P)[None, :]
    mask = np.where(col > row, MASKED, 0.0)
    e = np.arange(E)
    before = np.tile((e[None, :] < e[:, None]).astype(f32)[None], (P, 1, 1))
    return {"rope": rope.astype(f32), "ident": np.eye(P, dtype=f32), "mask_up": mask.astype(f32),
            "before": before}


def kernel(**inputs):
    import concourse.bacc as bacc
    from concourse.bass_utils import run_bass_kernel_spmd

    a = {k: np.asarray(v) for k, v in inputs.items()}
    swap = np.arange(D).reshape(NH, 2, HD // 2)[:, ::-1].reshape(D)
    wq, bq, wk, bk = (a[f"L0_attn_w{n}"] for n in ("q_w", "q_b", "k_w", "k_b"))
    arrays = {
        "x": a["L0_attn_x"],
        "w_in5": np.stack([wq, wq[:, swap], wk, wk[:, swap], a["L0_attn_wv_w"]], axis=1),
        "cols_in": np.stack([bq, bq[swap], bk, bk[swap], a["L0_attn_wo_b"]], axis=1),
        "bv": a["L0_attn_wv_b"],
        "wo": a["L0_attn_wo_w"],
        "wgT": a["L0_ffn_wg"].T,
        "w1T": a["L0_ffn_w1"].reshape(E * I, D).T,
        "w3T": a["L0_ffn_w3"].reshape(E * I, D).T,
        "w2T": a["L0_ffn_w2"].reshape(E, D, I // P, P).transpose(3, 0, 2, 1).reshape(P, E * I),
        "cT": a["L0_c"].T,
        "wmod": a["L0_wmod"],
        **constants(),
    }
    nc = bacc.Bacc("TRN2", target_bir_lowering=False, num_devices=1)
    feeds, args = {}, []
    for name, arr in arrays.items():
        arr = np.ascontiguousarray(arr)
        feeds[f"in_{name}"] = arr
        args.append(nc.dram_tensor(f"in_{name}", arr.shape, mybir.dt.from_np(arr.dtype), kind="ExternalInput").ap())
    args.append(nc.dram_tensor("out_0", (B, L, D), F32, kind="ExternalOutput").ap())
    build(nc, *args)
    return run_bass_kernel_spmd(nc, [feeds], core_ids=[0]).results[0]["out_0"]
```

```python
from contextlib import ExitStack

import numpy as np
import concourse.bass as bass
from concourse import mybir

F32 = mybir.dt.float32
F32R = mybir.dt.float32r
BF16 = mybir.dt.bfloat16
ALU = mybir.AluOpType
ACT = mybir.ActivationFunctionType
X = mybir.AxisListType.X
ds = bass.ds

P = 128
B, L, D = 4, 1024, 128
NH, HD = 16, 8
E, I = 8, 256
CH = 512
NCH = B * L // CH
NB = L // P
CB = CH // P
G = 4
UNITS = B * NH // G
NF = E * I // P
HR = P // G
SR = 3 * HD
ROWS = SR + 2
BUFS = 3
AHEAD = 4
SPLIT_AHEAD = 2
MASKED = -3.0e38
EPS = 1e-5
START = 1
SA, CA, GA, SB, CB_, GB = range(6)

SCORE_RING, MAX_RING = 3, 3
B_SCORES, B_CTX, B_MAX, B_MISC = 0, SCORE_RING, SCORE_RING + 1, 7


def key_steps():
    out = []
    for c in range(2):
        for kb in range(CB * (c + 1)):
            out.append((c, kb, max(0, kb - CB * c) * P))
    return out


KEYS = key_steps()
NQ = len(KEYS)
SLOTS = NQ * G
LEAD = 2 * G
CTX_EVAC = [G * q + LEAD for q in (CB - 1, NQ - 1)]
ACT_LEAD = CTX_EVAC[1] - SLOTS + 1
DIAGONAL = [q for q, (c, kb, _) in enumerate(KEYS) if kb >= CB * c]


def max_pieces():
    def heads_by(w):
        n = CH // w
        return [range(h, min(h + n, G)) for h in range(0, G, n)]

    out = []
    for qb in range(CB):
        w = (qb + 1) * P
        out += [(hs, qb, 0, w, 0) for hs in heads_by(w)]
    first = len(out)
    for qb in range(CB, NB):
        w = (qb - CB + 1) * P
        out += [(hs, qb, CH, w, 1) for hs in heads_by(w)] + [(hs, qb, 0, CH, 0) for hs in heads_by(CH)]
    return out, first


PIECES, FIRST_CHUNK_PIECES = max_pieces()
NP = len(PIECES)
NEG0_AT = FIRST_CHUNK_PIECES + 4
NEG0_READ_AT = NEG0_AT + 2
LAST_PIECE_BY = SLOTS - 8
NEG1_AT = SLOTS - 5


def pieces_before():
    time = []
    for n in range(LAST_PIECE_BY):
        score = CH - KEYS[(n + LEAD) % SLOTS // G][2]
        values = CH - KEYS[n // G][2]
        time.append(score + values + 500)
    cost = [64 + w * len(heads) for heads, _, _, w, _ in PIECES]
    m, spent, passed, out = 0, 0, 0, []
    for n in range(LAST_PIECE_BY):
        passed += time[n] / sum(time)
        while m < NP and spent < passed * sum(cost):
            spent += cost[m]
            m += 1
        out.append(m)
    return out[:-1] + [NP] * (SLOTS - LAST_PIECE_BY + 1)


BEFORE = pieces_before()
CTX0_AT = max(CTX_EVAC[0] - LEAD + 5, sum(m <= NEG0_READ_AT for m in BEFORE) + 3)


def build(nc, x, w_in5, cols_in, bv, wo, wgT, w1T, w3T, w2T, cT, wmod,
          rope, ident, mask_up, before, out):
    q_dram = nc.dram_tensor("q_split", (UNITS * G, ROWS, L), F32R, kind="Internal").ap()
    k_dram = nc.dram_tensor("k_split", (UNITS * G, SR, L), F32R, kind="Internal").ap()
    ew_dram = nc.dram_tensor("expert_w", (E, B * L), F32, kind="Internal").ap()

    with ExitStack() as ctx:
        def sb(name, shape, dt=F32, where=ctx):
            return where.enter_context(nc.sbuf_tensor(name, shape, dt))

        def sem(name):
            return ctx.enter_context(nc.semaphore(name))

        ps = ctx.enter_context(nc.psum_tensor("ps", [P, 8, CH], F32))

        x_sb = sb("x_sb", [P, B * NB, D])
        wo_sb, identf = sb("wo_sb", [P, D]), sb("identf", [P, P])
        identb = sb("identb", [P, P], BF16)
        maskb = sb("maskb", [P, P], BF16)
        beforej = sb("beforej", [P, E, E])
        wg_sb = sb("wg_sb", [P, E])
        cols = sb("cols", [P, 5])
        c_sb = sb("c_sb", [P, B])
        silu_c = sb("silu_c", [P, B])
        mod = sb("mod", [P, 6, B])
        gate_abs, gate_sign = sb("gate_abs", [P, B]), sb("gate_sign", [P, B])
        mod_now, mod_now2 = sb("mod_now", [P, 6]), sb("mod_now2", [P, 6])
        ga_now = sb("ga_now", [P, 1])
        gb_chunk, gb_now = sb("gb_chunk", [P, B, 2]), sb("gb_now", [P, 1])
        power = sb("power", [P, NB])
        stats, moments = sb("stats", [P, NB, 6]), sb("moments", [P, NB, 2])
        var_eps, rstd = sb("var_eps", [P, NB]), sb("rstd", [P, NB])
        logits = sb("logits", [P, NB, E])
        v_all = sb("v_all", [P, UNITS, NB, G * HD])
        ctx_all = sb("ctx_all", [P, UNITS, NB, G * HD])

        def region(*tenants):
            out, sizes = {}, []
            for t in tenants:
                stack = ExitStack()
                sizes.append((sum(int(np.prod(s[1:])) * (2 if d == BF16 else 4) for _, s, d in t), t))
                for name, shape, dt in t:
                    out[name] = sb(name, shape, dt, stack)
                stack.close()
            most = max(s for s, _ in sizes)
            sb(f"region_{len(regions)}", [P, most // 4])
            regions.append(most)
            return out

        regions = []
        k_shape = [P, G, L]
        r1 = region([(f"q{k}", [P, L], F32R) for k in range(BUFS)] + [(f"k{k}", k_shape, F32R) for k in range(2)],
                    [(f"{n}_{h}", [P, E * I], F32R) for n in ("w1", "w3", "w2") for h in ("hi", "lo")])
        q_s = [r1[f"q{k}"] for k in range(BUFS)]
        w1_hi, w1_lo, w3_hi, w3_lo, w2_hi, w2_lo = (r1[f"{n}_{h}"] for n in ("w1", "w3", "w2") for h in ("hi", "lo"))
        r2 = region([("probs", [P, BUFS, G, CH], F32), ("v_unit", [P, BUFS, NB, G, 32], F32)],
                    [("h2_hi", [P, B * L], F32R), ("h2_lo", [P, B * L], F32R),
                     ("y_sb", [P, CH], F32), ("o_sb", [P, CB, D], F32)])
        probs, v_unit, h2_hi, h2_lo, y_sb, o_sb = (
            r2[n] for n in ("probs", "v_unit", "h2_hi", "h2_lo", "y_sb", "o_sb"))
        r3 = region(
            [("rope_sb", [P, 2, L], F32), ("w_proj", [P, 5, D], F32), ("bv_sb", [P, D], F32), ("wmod_sb", [P, 6 * D], F32), ("mask_f", [P, P], F32),
             ("xn", [P, 2, CB, D], F32), ("h_t", [P, 2, CH], F32), ("rot1", [P, 2, CH], F32),
             ("rot2", [P, 2, CH], F32), ("qk_f", [P, 2, 2, CH], F32), ("qk_hi", [P, 2, 2, CH], F32R),
             ("qk_lo", [P, 2, 2, CH], F32R)],
            [("w_in", [P, 3, E * I], F32), ("ctx_st", [P, 2, CB, D], F32), ("ctx_t", [P, 2, CH], F32),
             ("att_t", [P, 2, CH], F32), ("xn2", [P, 2, CB, D], F32), ("h2_t", [P, 2, CH], F32),
             ("rank3", [P, NB, E, E], F32)],
            [("below_k2", [P, 3, E * I], F32), ("k2", k_shape, F32R)],
            [("wb", [P, E, CH], F32), ("s_f", [P, AHEAD, CH], F32), ("g_f", [P, AHEAD, CH], F32), ("gw_f", [P, AHEAD, CH], F32),
             ("g_hi", [P, AHEAD, CH], F32R), ("g_lo", [P, AHEAD, CH], F32R)])
        rope_sb, w_proj, bv_sb, wmod_sb, mask_f, xn, h_t, rot1, rot2, qk_f, qk_hi, qk_lo = (
            r3[n] for n in ("rope_sb", "w_proj", "bv_sb", "wmod_sb", "mask_f", "xn", "h_t", "rot1", "rot2", "qk_f", "qk_hi", "qk_lo"))
        k_s = [r1["k0"], r1["k1"], r3["k2"]]
        w_in, ctx_st, ctx_t, att_t, xn2, h2_t, rank3 = (
            r3[n] for n in ("w_in", "ctx_st", "ctx_t", "att_t", "xn2", "h2_t", "rank3"))
        wb, s_f, g_f, gw_f, g_hi, g_lo = (r3[n] for n in ("wb", "s_f", "g_f", "gw_f", "g_hi", "g_lo"))
        neg = sb("neg", [P, 2, G, CB])
        negm = sb("negm", [P, G, CB])
        neg_split = sb("neg_split", [P, 2, G, 2, CB], F32R)
        neg_t = sb("neg_t", [G * 2 * CB, 2, P], F32R)
        cat = sb("cat", [P, 2, CH])
        rsum = sb("rsum", [P, CB, G])
        eqs, chosen, lmax = sb("eqs", [P, NB, E]), sb("chosen", [P, NB, E]), sb("lmax", [P, NB])
        ew, ez = sb("ew", [P, NB, E]), sb("ez", [P, NB])
        expert_w = sb("expert_w_sb", [P, B * NB, E])
        ew_t = sb("ew_t", [P, 2, P])

        names = """waited mask_set w_loaded c_loaded x_loaded silu_c_done mod_mm mod_chain mod_done const_set
            ln_stats ln_moments ln_eps rstd_ready mod_cur xn_ready xt_done h_ready v_proj qk_proj rope_read
            qkf_ready hi_ready lo_ready v_evac scratch_written rows_zeroed rows_set zeros_written k2_set
            score_banks_free scores_ready probs_given_back mask_done v_staged units_done pieces_ready
            reduced neg_min neg_hi neg_lo neg_tp neg_evac ctx_evac ctx_tp sums_done ctx_finished
            ctx_staged ctx2_tp ctx2_evac att_mm att_evac att_tp x2_ready logit_mm logit_read h2hi_ready
            h2lo_ready w_in_loaded whi_ready wlo_ready route_chain lmax_sub ex_ready ewt_mm ewt_ready ew_written
            h_banks silu_done g_done gw_done ghi_done glo_done y_mm y_evac y_tp o_ready gb_cur ga_cur""".split()
        S = {n: sem(n) for n in names}
        qk_loaded = [sem(f"qk_loaded{k}") for k in range(BUFS)]
        neg_loaded = [sem(f"neg_loaded{c}") for c in range(2)]
        wb_loaded = [sem(f"wb_loaded{e}") for e in range(E)]
        out_written = sem("out_written")

        x_v = x.rearrange("b (n p) d -> p b n d", p=P)
        out_v = out.rearrange("b (n p) d -> p (b n) d", p=P)
        block = ctx.enter_context(nc.Block())
        UNIT_DMAS, NEG_DMAS = 8, 4
        ROUTE_STEPS = 12
        N_WEIGHT_DMAS = 9
        SPLIT_DMAS = 2 * 2 * 3

        def wait_alone(eng, semaphore, value):
            eng.wait_ge(semaphore, value)
            eng.sem_inc(S["waited"], 1)

        def norm_stats(dve, n0, done):
            for j in range(NB):
                last = nc.vector.bn_stats(stats[:, j, :], x_sb[:, ds(n0 + j, 1), :].rearrange("p a d -> p (a d)"))
            last.then_inc(S["ln_stats"], 1)
            wait_alone(dve, S["ln_stats"], done)
            for j in range(NB):
                last = nc.vector.bn_aggr(moments[:, j, :], stats[:, j, :])
            last.then_inc(S["ln_moments"], 1)

        def norm_rows(dve, n0, half, dst):
            for a in range(CB):
                j = CB * half + a
                last = nc.vector.tensor_scalar(
                    dst[:, half, a, :], x_sb[:, ds(n0 + j, 1), :].rearrange("p a d -> p (a d)"),
                    moments[:, j, 0:1], rstd[:, j:j + 1], ALU.subtract, ALU.mult)
            last.then_inc(S["xn_ready"], 1)

        def rstd_of(pool, done):
            wait_alone(pool, S["ln_moments"], done)
            nc.gpsimd.tensor_scalar(var_eps[:], moments[:, :, 1], EPS, None, ALU.add).then_inc(S["ln_eps"], 1)
            pool.wait_ge(S["ln_eps"], done)
            nc.gpsimd.tensor_tensor(rstd[:], var_eps[:], power[:], ALU.pow).then_inc(S["rstd_ready"], 1)

        from_start = [S[n] for n in """h_ready xt_done qk_proj qkf_ready lo_ready scratch_written v_evac
            rope_read ctx2_tp att_mm h2lo_ready logit_mm logit_read att_evac att_tp x2_ready ctx_tp
            ctx_finished ctx_evac y_evac o_ready""".split()] + neg_loaded + [out_written]

        @block.sync
        def _(sp):
            for semaphore in from_start:
                sp.sem_inc(semaphore, START)
            with sp.Fori(0, B) as b:
                sp.dma_start(x_sb[:, ds(b * NB, NB), :],
                             x_v[:, ds(b, 1)].rearrange("p a n d -> p (a n) d")).then_inc(S["x_loaded"], 16)
                wait_alone(sp, S["x_loaded"], 16 * b + 16)
            def save_batch(b):
                for k in range(2):
                    cs = slice(k * CH, (k + 1) * CH)
                    for s in range(2):
                        n = 4 * b + (2 * k + s + 1)
                        dst = (q_dram, k_dram)[s][ds(NH * b, NH)]
                        sp.wait_ge(S["hi_ready"], n)
                        for slot in ((0, 1), (0, 2))[s]:
                            sp.dma_start(dst[:, HD * slot:HD * (slot + 1), cs].bitcast(F32), qk_hi[:, s, k, :].bitcast(F32)
                                         ).then_inc(S["scratch_written"], 16)
                        sp.wait_ge(S["lo_ready"], n + START)
                        slot = (2, 1)[s]
                        sp.dma_start(dst[:, HD * slot:HD * (slot + 1), cs].bitcast(F32), qk_lo[:, s, k, :].bitcast(F32)
                                     ).then_inc(S["scratch_written"], 16)
            def load_unit(w, k):
                sp.wait_ge(S["units_done"], w + 1)
                for h in range(G):
                    q_src = q_dram[ds(G * w + h, 1)].rearrange("a r t -> (a r) t")
                    k_src = k_dram[ds(G * w + h, 1)].rearrange("a r t -> (a r) t")
                    sp.dma_start(q_s[k][HR * h:HR * h + ROWS, :].bitcast(F32), q_src.bitcast(F32)
                                 ).then_inc(qk_loaded[k], 16)
                    sp.dma_start(k_s[k][HR * h:HR * h + SR, h, :].bitcast(F32), k_src.bitcast(F32)
                                 ).then_inc(qk_loaded[k], 16)

            def load_neg(u, k, c):
                sp.wait_ge(S["neg_evac"], 2 * u + (c + 1))
                for h in range(G):
                    row_pair = q_s[k][HR * h + SR:HR * h + ROWS, c * CH:(c + 1) * CH].rearrange("r (q t) -> r q t", q=CB)
                    sp.dma_start(row_pair.bitcast(F32),
                                 neg_t[2 * CB * h:2 * CB * (h + 1), c, :].bitcast(F32)).then_inc(neg_loaded[c], 16)

            save_batch(0)
            sp.wait_ge(S["scratch_written"], 16 * SPLIT_DMAS + START)
            sp.wait_ge(S["zeros_written"], 16)
            sp.wait_ge(S["rows_set"], 1)
            for u in range(2):
                load_unit(u, u)
            with sp.Fori(1, B) as b:
                save_batch(b)
            sp.wait_ge(S["scratch_written"], 16 * SPLIT_DMAS * B + START)
            for c in range(2):
                load_neg(0, 0, c)
            for n, src in enumerate((w1T, w3T, w2T)):
                sp.dma_start(w_in[:, n, :], src).then_inc(S["w_in_loaded"], 16)
            sp.wait_ge(S["k2_set"], 1)
            LOOPED = (UNITS - 2) // BUFS
            with sp.Fori(0, LOOPED) as t:
                for k in range(BUFS):
                    load_unit(BUFS * t + (k + 2), (k + 2) % BUFS)
                    for c in range(2):
                        load_neg(BUFS * t + (k + 1), (k + 1) % BUFS, c)
            for u in range(BUFS * LOOPED, UNITS - 1):
                if u + 2 < UNITS:
                    load_unit(u + 2, (u + 2) % BUFS)
                for c in range(2):
                    load_neg(u + 1, (u + 1) % BUFS, c)

            sp.wait_ge(S["ewt_ready"], 1)
            for half in range(2):
                dst = ew_dram.rearrange("e (h n t) -> h n e t", h=2, n=2 * NB)[half]
                sp.dma_start(dst, ew_t[:, half, :]).then_inc(S["ew_written"], 16)
            sp.wait_ge(S["ew_written"], 32)
            sp.wait_ge(S["wlo_ready"], B)

            def load_wb(i, e):
                sp.dma_start(wb[:, e, :], ew_dram[e, ds(i * CH, CH)].partition_broadcast(P)).then_inc(wb_loaded[e], 16)

            def store(i):
                sp.wait_ge(S["o_ready"], i + 1 + START)
                sp.dma_start(out_v[:, ds(CB * i, CB), :], o_sb[:]).then_inc(out_written, 16)

            for e in range(E):
                load_wb(0, e)
            with sp.Fori(0, NCH - 1) as i:
                for e in range(E):
                    sp.wait_ge(S["gw_done"], NF * i + (2 * e + 2))
                    load_wb(i + 1, e)
                store(i)
            store(NCH - 1)
            sp.wait_ge(out_written, 16 * NCH + START)

        @block.gpsimd
        def _(pool):
            nc.gpsimd.memset(power[:], -0.5).then_inc(S["const_set"], 1)
            nc.gpsimd.memset(v_unit[:], 0.0).then_inc(S["const_set"], 1)
            pool.wait_ge(S["const_set"], 2)
            nc.gpsimd.memset(v_unit[:, :, :, :, HD:HD + 1], 1.0).then_inc(S["const_set"], 1)
            rstd_of(pool, 1)
            nc.gpsimd.memset(k_s[1][:].bitcast(F32), 0.0)
            for k in range(BUFS):
                last = nc.gpsimd.memset(q_s[k][:].bitcast(F32), 0.0)
            last.then_inc(S["rows_zeroed"], 1)
            pool.wait_ge(S["rows_zeroed"], 2)
            pool.wait_ge(S["zeros_written"], 16)
            for k in range(2):
                for h in range(G):
                    last = nc.gpsimd.memset(k_s[k][HR * h:HR * (h + 1), h, :].bitcast(F32), 1.0)
            last.then_inc(S["rows_set"], 1)
            pool.wait_ge(S["rows_set"], 1)

            rstd_of(pool, 2)

            def rotate(b, more=True):
                parts = [(k, s) for k in range(2) for s in range(2)]
                for at in range(len(parts) + 2):
                    if at < len(parts):
                        k, s = parts[at]
                        pool.wait_ge(S["rope_read"], 4 * b + (at + 1) + START)
                        pool.wait_ge(S["lo_ready"], 4 * b + START)
                        nc.gpsimd.tensor_tensor(qk_f[:, s, k, :], rot1[:, s, :], rot2[:, s, :], ALU.add
                                                ).then_inc(S["qkf_ready"], 1)
                    if at >= 2:
                        k, s = parts[at - 2]
                        pool.wait_ge(S["hi_ready"], 4 * b + (at - 1))
                        pool.wait_ge(S["scratch_written"], 16 * SPLIT_DMAS * b + START)
                        nc.gpsimd.tensor_tensor(qk_lo[:, s, k, :], qk_f[:, s, k, :], qk_hi[:, s, k, :].bitcast(F32),
                                                ALU.subtract).then_inc(S["lo_ready"], 1)
                if more:
                    rstd_of(pool, b + 3)

            with pool.Fori(0, B - 2) as b:
                rotate(b)
            for b in range(B - 2, B):
                rotate(b, more=False)

            def stage_v(w, k):
                pool.wait_ge(S["units_done"], w + 1)
                nc.gpsimd.tensor_copy(
                    v_unit[:, k, :, :, 0:HD],
                    v_all[:, ds(w, 1)].rearrange("p a n (h d) -> p (a n) h d", h=G)).then_inc(S["v_staged"], 1)

            def mask_diagonals(u, c):
                for q in DIAGONAL[CB * c:CB * (c + 1)]:
                    off = KEYS[q][2]
                    wait_alone(pool, S["score_banks_free"], SLOTS * u + (G * (q + 1) + SCORE_RING))
                    tile = probs[:, q % BUFS, :, off:off + P]
                    nc.gpsimd.affine_select(out=tile, in_=tile, compare_op=ALU.is_ge, fill=0.0, base=0,
                                            pattern=[[0, G], [1, P]], channel_multiplier=-1
                                            ).then_inc(S["mask_done"], 1)

            pool.wait_ge(S["v_evac"], NCH + START)
            pool.wait_ge(S["const_set"], 3)
            stage_v(0, 0)
            with pool.Fori(0, (UNITS - 1) // BUFS) as t:
                for k in range(BUFS):
                    mask_diagonals(BUFS * t + k, 0)
                    stage_v(BUFS * t + (k + 1), (k + 1) % BUFS)
                    mask_diagonals(BUFS * t + k, 1)
            for c in range(2):
                mask_diagonals(UNITS - 1, c)

            pool.wait_ge(S["ctx_finished"], 2 * UNITS + START)
            pool.wait_ge(S["w_in_loaded"], 48)
            def stage_context(b):
                for k in range(2):
                    pool.wait_ge(S["ctx2_tp"], 2 * b + START)
                    for g in range(NH // G):
                        last = nc.gpsimd.tensor_copy(
                            ctx_st[:, k, :, g * G * HD:(g + 1) * G * HD],
                            ctx_all[:, ds(4 * b + g, 1), CB * k:CB * (k + 1), :].rearrange("p a n d -> p (a n) d"))
                    last.then_inc(S["ctx_staged"], 1)

            def weights_lo(b):
                pool.wait_ge(S["whi_ready"], b + 1)
                for n, (hi, lo) in enumerate(((w1_hi, w1_lo), (w3_hi, w3_lo), (w2_hi, w2_lo))):
                    last = nc.gpsimd.tensor_tensor(lo[:, ds(b * CH, CH)], w_in[:, n, ds(b * CH, CH)],
                                                   hi[:, ds(b * CH, CH)].bitcast(F32), ALU.subtract)
                last.then_inc(S["wlo_ready"], 1)

            def h2_lo_of(b):
                for k in range(2):
                    pool.wait_ge(S["h2hi_ready"], 2 * b + (k + 1))
                    nc.gpsimd.tensor_tensor(h2_lo[:, ds((2 * b + k) * CH, CH)], h2_t[:, k, :],
                                            h2_hi[:, ds((2 * b + k) * CH, CH)].bitcast(F32), ALU.subtract
                                            ).then_inc(S["h2lo_ready"], 1)

            stage_context(0)
            stage_context(1)
            rstd_of(pool, B + 1)
            with pool.Fori(1, B - 1) as b:
                stage_context(b + 1)
                weights_lo(b - 1)
                h2_lo_of(b - 1)
                rstd_of(pool, B + b + 1)
            weights_lo(B - 2)
            h2_lo_of(B - 2)
            rstd_of(pool, 2 * B)
            weights_lo(B - 1)
            h2_lo_of(B - 1)

            with pool.Fori(0, NCH) as i:
                for f in range(NF):
                    if f % 2 == 0:
                        pool.wait_ge(wb_loaded[f // 2], 16 * i + 16)
                    pool.wait_ge(S["g_done"], NF * i + (f + 1))
                    nc.gpsimd.tensor_tensor(gw_f[:, f % AHEAD, :], g_f[:, f % AHEAD, :], wb[:, f // 2, :], ALU.mult
                                            ).then_inc(S["gw_done"], 1)

        @block.scalar
        def _(act):
            act.dma_start(c_sb[:], cT).then_inc(S["c_loaded"], 16)
            act.dma_start(wmod_sb[:], wmod).then_inc(S["c_loaded"], 16)
            for dst, src in ((w_proj[:], w_in5), (cols[:], cols_in), (identf[:], ident), (mask_f[:], mask_up),
                             (rope_sb[:], rope), (wo_sb[:], wo), (wg_sb[:], wgT),
                             (bv_sb[:], bv.partition_broadcast(P))):
                act.dma_start(dst, src).then_inc(S["w_loaded"], 16)
            act.dma_start(beforej[:], before).then_inc(S["w_loaded"], 16)
            act.wait_ge(S["rows_zeroed"], 1)
            act.dma_start(q_dram[:, SR:ROWS, :].bitcast(F32),
                          k_s[0][0:UNITS * G, 0:2, :].bitcast(F32)).then_inc(S["zeros_written"], 16)
            act.sem_inc(S["score_banks_free"], SCORE_RING)
            act.wait_ge(S["c_loaded"], 32)
            nc.scalar.activation(silu_c[:], c_sb[:], ACT.Silu).then_inc(S["silu_c_done"], 1)

            act.wait_ge(S["mod_done"], 1)
            def modulate(b, k):
                if k == 0:
                    act.wait_ge(S["mod_cur"], b + 1)
                act.wait_ge(S["xt_done"], 2 * b + (k + 1) + START)
                nc.scalar.activation(h_t[:, k, :], ps[:, k, :], ACT.Identity, bias=mod_now[:, SA:SA + 1],
                                     scale=mod_now[:, CA:CA + 1]).then_inc(S["h_ready"], 1)

            def keep_hi_of(b, k):
                for s in range(2):
                    act.wait_ge(S["qkf_ready"], 4 * b + (2 * k + s + 1) + START)
                    act.wait_ge(S["scratch_written"], 16 * SPLIT_DMAS * b + START)
                    nc.scalar.activation(qk_hi[:, s, k, :], qk_f[:, s, k, :], ACT.Copy).then_inc(S["hi_ready"], 1)

            for k in range(2):
                modulate(0, k)
            with act.Fori(0, B - 1) as b:
                keep_hi_of(b, 0)
                for k in range(2):
                    act.wait_ge(S["qk_proj"], 4 * b + 2 * (k + 1) + START)
                    modulate(b + 1, k)
                keep_hi_of(b, 1)
            for k in range(2):
                keep_hi_of(B - 1, k)

            def exp(u, n):
                q, h = divmod(n, G)
                off = KEYS[q][2]
                act.wait_ge(S["scores_ready"], SLOTS * u + (n + 1))
                if h == 0:
                    act.wait_ge(S["probs_given_back"], NQ * u + (q + 1))
                nc.scalar.activation(probs[:, q % BUFS, h, off:], ps[:, B_SCORES + n % SCORE_RING, off:],
                                     ACT.Exp, scale=float(HD) ** -0.5).then_inc(S["score_banks_free"], 1)

            def evacuate_context(u, c):
                act.wait_ge(S["probs_given_back"], NQ * u + (BUFS + (CB, NQ)[c]))
                act.wait_ge(S["ctx_tp"], 2 * u + START)
                nc.scalar.activation(cat[:, c, :], ps[:, B_CTX, :], ACT.Copy).then_inc(S["ctx_evac"], 1)

            def unit(u, last=False):
                for n in range(ACT_LEAD, SLOTS + ACT_LEAD):
                    if n < SLOTS:
                        exp(u, n)
                    elif not last:
                        exp(u + 1, n - SLOTS)
                    if n in CTX_EVAC:
                        evacuate_context(u, CTX_EVAC.index(n))

            for n in range(ACT_LEAD):
                exp(0, n)
            with act.Fori(0, (UNITS - 1) // BUFS) as t:
                for k in range(BUFS):
                    unit(BUFS * t + k)
            unit(UNITS - 1, last=True)

            act.wait_ge(S["w_in_loaded"], 48)
            act.wait_ge(S["ctx_finished"], 2 * UNITS + START)
            def evacuate_ctx2(b):
                for k in range(2):
                    act.wait_ge(S["ctx2_tp"], 2 * b + (k + 1) + START)
                    act.wait_ge(S["att_mm"], 2 * b + START)
                    nc.scalar.activation(ctx_t[:, k, :], ps[:, k, :], ACT.Copy).then_inc(S["ctx2_evac"], 1)

            def weights_hi(b):
                for n, hi in enumerate((w1_hi, w3_hi, w2_hi)):
                    last = nc.scalar.activation(hi[:, ds(b * CH, CH)], w_in[:, n, ds(b * CH, CH)], ACT.Copy)
                last.then_inc(S["whi_ready"], 1)

            def modulate_h2(b):
                act.wait_ge(S["mod_cur"], B + b + 1)
                for k in range(2):
                    act.wait_ge(S["xt_done"], NCH + 2 * b + (k + 1) + START)
                    act.wait_ge(S["h2lo_ready"], 2 * b + START)
                    act.wait_ge(S["logit_mm"], 2 * b + START)
                    nc.scalar.activation(h2_t[:, k, :], ps[:, 6 + k, :], ACT.Identity, bias=mod_now2[:, SB:SB + 1],
                                         scale=mod_now2[:, CB_:CB_ + 1]).then_inc(S["h_ready"], 1)
                for k in range(2):
                    act.wait_ge(S["h_ready"], NCH + 2 * b + (k + 1) + START)
                    nc.scalar.activation(h2_hi[:, ds((2 * b + k) * CH, CH)], h2_t[:, k, :], ACT.Copy
                                         ).then_inc(S["h2hi_ready"], 1)

            def router_exp(b):
                act.wait_ge(S["lmax_sub"], b + 1)
                nc.scalar.activation(ew[:], ew[:], ACT.Exp).then_inc(S["ex_ready"], 1)

            evacuate_ctx2(0)
            weights_hi(0)
            with act.Fori(1, B) as b:
                evacuate_ctx2(b)
                modulate_h2(b - 1)
                weights_hi(b)
                router_exp(b - 1)
            modulate_h2(B - 1)
            router_exp(B - 1)

            def silu(i, f):
                act.wait_ge(S["h_banks"], NF * i + (f + 1))
                nc.scalar.activation(s_f[:, f % AHEAD, :], ps[:, 2 * (f % 2), :], ACT.Silu).then_inc(S["silu_done"], 1)

            def keep_hi(i, f):
                act.wait_ge(S["gw_done"], NF * i + (f + 1))
                nc.scalar.activation(g_hi[:, f % AHEAD, :], gw_f[:, f % AHEAD, :], ACT.Copy).then_inc(S["ghi_done"], 1)

            def chunk(i, last=False):
                for f in range(NF):
                    if f + SPLIT_AHEAD < NF:
                        keep_hi(i, f + SPLIT_AHEAD)
                    elif not last:
                        keep_hi(i + 1, f + SPLIT_AHEAD - NF)
                    if f + AHEAD < NF:
                        silu(i, f + AHEAD)
                    elif not last:
                        silu(i + 1, f + AHEAD - NF)

            for f in range(AHEAD):
                silu(0, f)
            for f in range(SPLIT_AHEAD):
                keep_hi(0, f)
            with act.Fori(0, NCH - 1) as i:
                chunk(i)
            chunk(NCH - 1, last=True)

        @block.vector
        def _(dve):
            nc.vector.memset(k_s[0][:].bitcast(F32), 0.0).then_inc(S["rows_zeroed"], 1)
            dve.wait_ge(S["x_loaded"], 16)
            norm_stats(dve, 0, 1)
            dve.wait_ge(S["mod_mm"], 1)
            nc.vector.tensor_copy(mod[:].rearrange("p s b -> p (s b)"), ps[:, 7, 0:6 * B]).then_inc(S["mod_chain"], 1)
            dve.wait_ge(S["mod_chain"], 1)
            for slot in (CA, CB_):
                nc.vector.tensor_scalar(mod[:, slot, :], mod[:, slot, :], 1.0, None, ALU.add)
            n = 1
            for slot in (GA, GB):
                nc.vector.tensor_scalar(gate_sign[:], mod[:, slot, :], 0.0, 2.0, ALU.is_ge, ALU.mult)
                nc.vector.scalar_tensor_tensor(gate_abs[:], mod[:, slot, :], -1.0, mod[:, slot, :], ALU.mult, ALU.max
                                               ).then_inc(S["mod_chain"], 1)
                n += 1
                dve.wait_ge(S["mod_chain"], n)
                nc.vector.tensor_scalar(gate_abs[:], gate_abs[:], 0.25, None, ALU.max).then_inc(S["mod_chain"], 1)
                n += 1
                dve.wait_ge(S["mod_chain"], n)
                nc.vector.scalar_tensor_tensor(mod[:, slot, :], gate_sign[:], -1.0, gate_abs[:], ALU.add, ALU.mult
                                               ).then_inc(S["mod_chain"], 1)
                n += 1
                dve.wait_ge(S["mod_chain"], n)
            for k in range(2):
                last = nc.vector.tensor_copy(gb_chunk[:, :, k], mod[:, GB, :])
            last.then_inc(S["mod_done"], 1)
            dve.wait_ge(S["mod_done"], 1)

            dve.wait_ge(S["w_loaded"], 16 * N_WEIGHT_DMAS)
            nc.vector.tensor_copy(identb[:], identf[:])
            nc.vector.tensor_copy(maskb[:], mask_f[:]).then_inc(S["mask_set"], 1)
            def prepare(b):
                dve.wait_ge(S["h_ready"], 2 * b + START)
                nc.vector.tensor_copy(mod_now[:], mod[:, :, ds(b, 1)].rearrange("p s a -> p (s a)")
                                      ).then_inc(S["mod_cur"], 1)
                dve.wait_ge(S["rstd_ready"], b + 1)
                dve.wait_ge(S["xt_done"], 2 * b + START)
                for k in range(2):
                    norm_rows(dve, NB * b, k, xn)

            def next_stats(b):
                dve.wait_ge(S["xn_ready"], 2 * b + 2)
                wait_alone(dve, S["x_loaded"], 16 * (b + 1) + 16)
                norm_stats(dve, NB * (b + 1), b + 2)

            def values_and_rotation(b, k):
                cs = slice(k * CH, (k + 1) * CH)
                dve.wait_ge(S["v_proj"], 2 * b + (k + 1))
                for a in range(CB):
                    last = nc.vector.tensor_tensor(
                        v_all[:, ds(4 * b, 4), CB * k + a, :],
                        ps[:, 6 + k, a * P:(a + 1) * P].rearrange("p (g d) -> p g d", g=4),
                        bv_sb[:].rearrange("p (g d) -> p g d", g=4), ALU.add)
                last.then_inc(S["v_evac"], 1)
                for s in range(2):
                    dve.wait_ge(S["qk_proj"], 4 * b + (2 * k + s + 1) + START)
                    dve.wait_ge(S["qkf_ready"], 4 * b + (k * (s + 1)) + START)
                    nc.vector.scalar_tensor_tensor(rot1[:, s, :], ps[:, 2 + 2 * s, :], cols[:, 2 * s:2 * s + 1],
                                                   rope_sb[:, 0, cs], ALU.add, ALU.mult)
                    nc.vector.scalar_tensor_tensor(rot2[:, s, :], ps[:, 3 + 2 * s, :],
                                                   cols[:, 2 * s + 1:2 * s + 2], rope_sb[:, 1, cs], ALU.add,
                                                   ALU.mult).then_inc(S["rope_read"], 1)

            def batch(b, prepare_next=True, stats_after=True):
                values_and_rotation(b, 0)
                if prepare_next:
                    prepare(b + 1)
                values_and_rotation(b, 1)
                if stats_after:
                    next_stats(b + 1)

            prepare(0)
            next_stats(0)
            with dve.Fori(0, B - 2) as b:
                batch(b)
            batch(B - 2, stats_after=False)
            batch(B - 1, prepare_next=False, stats_after=False)

            def reduce_piece(m, v, k):
                heads, qb, _, w, part = PIECES[m]
                n = len(heads)
                dve.wait_ge(S["pieces_ready"], NP * v + (m + 1))
                nc.vector.tensor_reduce(neg[:, part, heads[0]:heads[-1] + 1, qb % CB],
                                        ps[:, B_MAX + (NP * k + m) % MAX_RING, 0:n * w].rearrange("p (n w) -> p n w", n=n),
                                        axis=X, op=ALU.max, negate=True).then_inc(S["reduced"], 1)

            def split_neg(c, v):
                dst = neg_split[:, c]
                src = neg[:, 0]
                dve.wait_ge(S["reduced"], NP * v + (NP if c else FIRST_CHUNK_PIECES))
                if c:
                    nc.vector.tensor_tensor(negm[:], neg[:, 0], neg[:, 1], ALU.min).then_inc(S["neg_min"], 1)
                    dve.wait_ge(S["neg_min"], v + 1)
                    src = negm[:]
                nc.vector.tensor_copy(dst[:, :, 0, :], src).then_inc(S["neg_hi"], 1)
                dve.wait_ge(S["neg_hi"], 2 * v + (c + 1))
                nc.vector.tensor_tensor(dst[:, :, 1, :], src, dst[:, :, 0, :].bitcast(F32), ALU.subtract
                                        ).then_inc(S["neg_lo"], 1)

            def read_neg(c, v):
                dve.wait_ge(S["neg_tp"], 2 * v + (c + 1))
                dve.wait_ge(neg_loaded[c], 16 * NEG_DMAS * v + START)
                nc.vector.tensor_copy(neg_t[:, c, :], ps[0:G * 2 * CB, B_MISC, 0:P]).then_inc(S["neg_evac"], 1)

            def finish_context(c, u):
                heads = ps[:, B_MISC, :].rearrange("p (a h r) -> p a h r", a=CB, h=G)
                dve.wait_ge(S["ctx_tp"], 2 * u + (c + 1) + START)
                nc.vector.reciprocal(rsum[:], heads[:, :, :, HD]).then_inc(S["sums_done"], 1)
                dve.wait_ge(S["sums_done"], 2 * u + (c + 1))
                nc.vector.tensor_tensor(
                    ctx_all[:, ds(u, 1), CB * c:CB * (c + 1), :].rearrange("p a n (h d) -> p (a n) h d", h=G),
                    heads[:, :, :, 0:HD], rsum[:].unsqueeze(3).broadcast_to([P, CB, G, HD]), ALU.mult
                ).then_inc(S["ctx_finished"], 1)

            def maxima(v, k, m):
                if m == FIRST_CHUNK_PIECES:
                    split_neg(0, v)
                if m == FIRST_CHUNK_PIECES + 1:
                    dve.wait_ge(S["neg_lo"], 2 * v + 1)
                if m == NEG0_READ_AT:
                    read_neg(0, v)
                reduce_piece(m, v, k)
                if m == NP - 1:
                    split_neg(1, v)

            def unit(u, k, last=False):
                for n in range(SLOTS):
                    if not last:
                        for m in range(BEFORE[n - 1] if n else 0, BEFORE[n]):
                            maxima(u + 1, (k + 1) % BUFS, m)
                        if n == NEG1_AT + 1:
                            read_neg(1, u + 1)
                    if n == CTX0_AT + 1:
                        finish_context(0, u)
                finish_context(1, u)

            for m in range(NP):
                maxima(0, 0, m)
            read_neg(1, 0)
            dve.wait_ge(S["scratch_written"], 16 * SPLIT_DMAS * B + START)
            nc.vector.memset(k_s[2][:].bitcast(F32), 0.0).then_inc(S["rows_zeroed"], 1)
            dve.wait_ge(S["rows_zeroed"], 3)
            for h in range(G):
                last = nc.vector.memset(k_s[2][HR * h:HR * (h + 1), h, :].bitcast(F32), 1.0)
            last.then_inc(S["k2_set"], 1)
            with dve.Fori(0, (UNITS - 1) // BUFS) as t:
                for k in range(BUFS):
                    unit(BUFS * t + k, k)
            unit(UNITS - 1, 0, last=True)

            def attention_residual(b):
                nc.vector.tensor_copy(ga_now[:], mod[:, GA, ds(b, 1)]).then_inc(S["ga_cur"], 1)
                dve.wait_ge(S["ga_cur"], b + 1)
                for k in range(2):
                    dve.wait_ge(S["att_mm"], 2 * b + (k + 1) + START)
                    dve.wait_ge(S["att_tp"], 2 * b + START)
                    nc.vector.tensor_scalar(att_t[:, k, :], ps[:, 2 + k, :], cols[:, 4:5], ga_now[:, 0:1],
                                            ALU.add, ALU.mult).then_inc(S["att_evac"], 1)

            def second_norm_stats(b):
                for k in range(2):
                    rows = x_sb[:, ds(NB * b + CB * k, CB), :]
                    dve.wait_ge(S["att_tp"], 2 * b + (k + 1) + START)
                    nc.vector.tensor_tensor(rows, ps[:, 4 + k, :].rearrange("p (a d) -> p a d", a=CB), rows, ALU.add
                                            ).then_inc(S["x2_ready"], 1)
                dve.wait_ge(S["xn_ready"], NCH + 2 * b)
                wait_alone(dve, S["x2_ready"], 2 * b + 2 + START)
                norm_stats(dve, NB * b, B + b + 1)

            def second_norm_rows(b):
                dve.wait_ge(S["h_ready"], NCH + 2 * b + START)
                nc.vector.tensor_copy(mod_now2[:], mod[:, :, ds(b, 1)].rearrange("p s a -> p (s a)")
                                      ).then_inc(S["mod_cur"], 1)
                dve.wait_ge(S["rstd_ready"], B + b + 1)
                dve.wait_ge(S["xt_done"], NCH + 2 * b + START)
                for k in range(2):
                    norm_rows(dve, NB * b, k, xn2)

            def read_logits(b):
                for k in range(2):
                    dve.wait_ge(S["logit_mm"], 2 * b + (k + 1) + START)
                    nc.vector.tensor_copy(logits[:, CB * k:CB * (k + 1), :],
                                          ps[:, k, 0:CB * E].rearrange("p (a e) -> p a e", a=CB)
                                          ).then_inc(S["logit_read"], 1)

            def router(b):
                step = [0]

                def chained(ins):
                    step[0] += 1
                    ins.then_inc(S["route_chain"], 1)
                    dve.wait_ge(S["route_chain"], ROUTE_STEPS * b + step[0])

                dve.wait_ge(S["logit_read"], 2 * b + 2 + START)
                by_e = logits[:].unsqueeze(3).broadcast_to([P, NB, E, E])
                by_j = logits[:].unsqueeze(2).broadcast_to([P, NB, E, E])
                chained(nc.vector.reduce_max(lmax[:], logits[:], axis=X))
                nc.vector.tensor_tensor(ew[:], logits[:], lmax[:].unsqueeze(2).broadcast_to([P, NB, E]), ALU.subtract
                                        ).then_inc(S["lmax_sub"], 1)
                chained(nc.vector.tensor_tensor(rank3[:], by_j, by_e, ALU.is_equal))
                chained(nc.vector.tensor_tensor(rank3[:], rank3[:],
                                                beforej[:].unsqueeze(1).broadcast_to([P, NB, E, E]), ALU.mult))
                chained(nc.vector.reduce_sum(eqs[:], rank3[:], axis=X))
                chained(nc.vector.tensor_tensor(rank3[:], by_j, by_e, ALU.is_gt))
                chained(nc.vector.reduce_sum(chosen[:], rank3[:], axis=X))
                chained(nc.vector.tensor_tensor(chosen[:], chosen[:], eqs[:], ALU.add))
                chained(nc.vector.tensor_scalar(chosen[:], chosen[:], 1.5, None, ALU.is_lt))
                dve.wait_ge(S["ex_ready"], b + 1)
                chained(nc.vector.tensor_tensor(ew[:], ew[:], chosen[:], ALU.mult))
                chained(nc.vector.reduce_sum(ez[:], ew[:], axis=X))
                chained(nc.vector.reciprocal(ez[:], ez[:]))
                chained(nc.vector.tensor_tensor(expert_w[:, ds(NB * b, NB), :], ew[:],
                                                ez[:].unsqueeze(2).broadcast_to([P, NB, E]), ALU.mult))
                assert step[0] == ROUTE_STEPS

            attention_residual(0)
            second_norm_stats(0)
            with dve.Fori(1, B) as b:
                second_norm_rows(b - 1)
                attention_residual(b)
                second_norm_stats(b)
                read_logits(b - 1)
                router(b - 1)
            second_norm_rows(B - 1)
            read_logits(B - 1)
            router(B - 1)
            dve.wait_ge(S["ewt_mm"], 1)
            nc.vector.tensor_copy(ew_t[:], ps[:, 5, 0:2 * P].rearrange("p (h t) -> p h t", h=2)
                                  ).then_inc(S["ewt_ready"], 1)

            def gate(i, f):
                dve.wait_ge(S["silu_done"], NF * i + (f + 1))
                nc.vector.tensor_tensor(g_f[:, f % AHEAD, :], ps[:, 2 * (f % 2) + 1, :], s_f[:, f % AHEAD, :], ALU.mult
                                        ).then_inc(S["g_done"], 1)

            def keep_lo(i, f):
                dve.wait_ge(S["ghi_done"], NF * i + (f + 1))
                nc.vector.tensor_tensor(g_lo[:, f % AHEAD, :], gw_f[:, f % AHEAD, :], g_hi[:, f % AHEAD, :].bitcast(F32),
                                        ALU.subtract).then_inc(S["glo_done"], 1)

            def chunk(i, last=False):
                nc.vector.tensor_copy(gb_now[:], gb_chunk[:].rearrange("p b k -> p (b k)")[:, ds(i, 1)]
                                      ).then_inc(S["gb_cur"], 1)
                for f in range(NF):
                    if f + SPLIT_AHEAD < NF:
                        keep_lo(i, f + SPLIT_AHEAD)
                    elif not last:
                        keep_lo(i + 1, f + SPLIT_AHEAD - NF)
                    if f == NF - 1:
                        dve.wait_ge(S["gb_cur"], i + 1)
                        dve.wait_ge(S["y_mm"], i + 1)
                        nc.vector.tensor_scalar(y_sb[:], ps[:, 4, :], gb_now[:, 0:1], None, ALU.mult
                                                ).then_inc(S["y_evac"], 1)
                    if f + AHEAD < NF:
                        gate(i, f + AHEAD)
                    elif not last:
                        gate(i + 1, f + AHEAD - NF)
                dve.wait_ge(S["y_tp"], i + 1)
                dve.wait_ge(out_written, 16 * i + START)
                nc.vector.tensor_tensor(o_sb[:], ps[:, 5, :].rearrange("p (a d) -> p a d", a=CB),
                                        x_sb[:, ds(CB * i, CB), :], ALU.add).then_inc(S["o_ready"], 1)

            for f in range(AHEAD):
                gate(0, f)
            for f in range(SPLIT_AHEAD):
                keep_lo(0, f)
            with dve.Fori(0, NCH - 1) as i:
                chunk(i)
            chunk(NCH - 1, last=True)

        @block.tensor
        def _(pe):
            mm, tp = nc.tensor.matmul, nc.tensor.transpose
            pe.sem_inc(S["probs_given_back"], BUFS)
            pe.sem_inc(S["units_done"], BUFS)
            pe.wait_ge(S["silu_c_done"], 1)
            for slot in range(6):
                last = mm(ps[:, 7, slot * B:(slot + 1) * B], wmod_sb[:, slot * D:(slot + 1) * D], silu_c[:],
                          start=True, stop=True)
            last.then_inc(S["mod_mm"], 1)

            pe.wait_ge(S["w_loaded"], 16 * N_WEIGHT_DMAS)
            pe.wait_ge(S["mask_set"], 1)
            pe.wait_ge(S["mod_done"], 1)
            def turn_rows(b):
                pe.wait_ge(S["h_ready"], 2 * b + START)
                for k in range(2):
                    pe.wait_ge(S["xn_ready"], 2 * b + (k + 1))
                    for a in range(CB):
                        last = tp(ps[:, k, a * P:(a + 1) * P], xn[:, k, a, :], identf[:])
                    last.then_inc(S["xt_done"], 1)

            def project(b):
                pe.wait_ge(S["v_evac"], 2 * b + START)
                for k in range(2):
                    pe.wait_ge(S["h_ready"], 2 * b + (k + 1) + START)
                    for a in range(CB):
                        last = mm(ps[:, 6 + k, a * P:(a + 1) * P], h_t[:, k, a * P:(a + 1) * P], w_proj[:, 4, :],
                                  start=True, stop=True)
                    last.then_inc(S["v_proj"], 1)
                    pe.wait_ge(S["rope_read"], 4 * b + 2 * k + START)
                    for s in range(2):
                        mm(ps[:, 2 + 2 * s, :], w_proj[:, 2 * s, :], h_t[:, k, :], start=True, stop=True)
                        mm(ps[:, 3 + 2 * s, :], w_proj[:, 2 * s + 1, :], h_t[:, k, :], start=True, stop=True
                           ).then_inc(S["qk_proj"], 1)

            turn_rows(0)
            with pe.Fori(0, B - 1) as b:
                project(b)
                turn_rows(b + 1)
            project(B - 1)

            def max_piece(m, v, k, first=False):
                heads, qb, c0, w, part = PIECES[m]
                if not first or m >= MAX_RING:
                    pe.wait_ge(S["reduced"], NP * v + (m - MAX_RING + 1))
                bank = B_MAX + (NP * k + m) % MAX_RING
                for n, h in enumerate(heads):
                    last = mm(ps[:, bank, n * w:(n + 1) * w], q_s[k][:, qb * P:(qb + 1) * P],
                              k_s[k][:, h, c0:c0 + w], start=True, stop=True)
                    if part == 1 or qb < CB:
                        last = mm(ps[:, bank, (n + 1) * w - P:(n + 1) * w], identb[:], maskb[:],
                                  start=False, stop=True, skip_group_check=True)
                last.then_inc(S["pieces_ready"], 1)

            def turn_neg(c, v):
                pe.wait_ge(S["neg_lo"], 2 * v + (c + 1))
                tp(ps[0:G * 2 * CB, B_MISC, 0:P], neg_split[:, c].rearrange("p h s q -> p (h s q)").bitcast(F32), identf[:]
                   ).then_inc(S["neg_tp"], 1)

            def turn_context(c, u):
                pe.wait_ge(S["ctx_evac"], 2 * u + (c + 1) + START)
                for a in range(CB):
                    last = tp(ps[:, B_MISC, a * P:(a + 1) * P], cat[:, c, a * P:(a + 1) * P], identf[:])
                last.then_inc(S["ctx_tp"], 1)

            def weigh_values(q, u, k):
                c, kb, off = KEYS[q]
                if q in DIAGONAL:
                    pe.wait_ge(S["mask_done"], len(DIAGONAL) * u + (DIAGONAL.index(q) + 1))
                else:
                    pe.wait_ge(S["score_banks_free"], SLOTS * u + (G * (q + 1) + SCORE_RING))
                if kb == 0:
                    pe.wait_ge(S["v_staged"], u + 1)
                    pe.wait_ge(S["ctx_evac"], 2 * u + c + START)
                for h in range(G):
                    last = mm(ps[32 * h:32 * h + 32, B_CTX, off:], v_unit[:, k, kb, h, :],
                              probs[:, q % BUFS, h, off:], start=kb == 0, stop=kb == CB * (c + 1) - 1)
                    if q == NQ - 1 and h == G - 2:
                        last.then_inc(S["units_done"], 1)
                last.then_inc(S["probs_given_back"], 1)

            def score(u, k, n):
                q, h = divmod(n, G)
                c, kb, off = KEYS[q]
                if kb == h == 0:
                    pe.wait_ge(neg_loaded[c], 16 * NEG_DMAS * (u + 1) + START)
                pe.wait_ge(S["score_banks_free"], SLOTS * u + (n + 1))
                mm(ps[:, B_SCORES + n % SCORE_RING, off:], k_s[k][:, h, kb * P:(kb + 1) * P],
                   q_s[k][:, c * CH + off:(c + 1) * CH], start=True, stop=True).then_inc(S["scores_ready"], 1)

            def unit(u, t, k, last=False):
                km = (k + 1) % BUFS
                if not last:
                    pe.wait_ge(qk_loaded[km], 16 * UNIT_DMAS * (t + (1 if km else 2)))
                for n in range(SLOTS):
                    if n + LEAD < SLOTS:
                        score(u, k, n + LEAD)
                    elif not last:
                        score(u + 1, km, n + LEAD - SLOTS)
                    if not last:
                        for m in range(BEFORE[n - 1] if n else 0, BEFORE[n]):
                            if m == NEG0_AT:
                                pe.wait_ge(S["ctx_finished"], 2 * u + START)
                                turn_neg(0, u + 1)
                            max_piece(m, u + 1, km)
                        if n == NEG1_AT:
                            pe.wait_ge(S["ctx_finished"], 2 * u + 1 + START)
                            turn_neg(1, u + 1)
                    if n % G == 0:
                        weigh_values(n // G, u, k)
                    if n in (CTX0_AT, SLOTS - 1):
                        c = int(n == SLOTS - 1)
                        if last:
                            pe.wait_ge(S["ctx_finished"], 2 * u + c + START)
                        else:
                            pe.wait_ge(S["neg_evac"], 2 * u + (3 + c))
                        turn_context(c, u)

            pe.wait_ge(S["v_evac"], NCH + START)
            pe.wait_ge(S["rope_read"], 4 * B + START)
            pe.wait_ge(qk_loaded[0], 16 * UNIT_DMAS)
            for m in range(NP):
                if m == NEG0_AT:
                    turn_neg(0, 0)
                max_piece(m, 0, 0, first=True)
            pe.wait_ge(S["neg_evac"], 1)
            turn_neg(1, 0)
            for n in range(LEAD):
                score(0, 0, n)
            with pe.Fori(0, (UNITS - 1) // BUFS) as t:
                for k in range(BUFS):
                    unit(BUFS * t + k, t, k)
            unit(UNITS - 1, (UNITS - 1) // BUFS, 0, last=True)

            pe.wait_ge(S["ctx_finished"], 2 * UNITS + START)
            def turn_ctx2(b, first=False):
                if not first:
                    pe.wait_ge(S["logit_read"], 2 * (b - 1) + START)
                for k in range(2):
                    pe.wait_ge(S["ctx_staged"], 2 * b + (k + 1))
                    for a in range(CB):
                        last = tp(ps[:, k, a * P:(a + 1) * P], ctx_st[:, k, a, :], identf[:])
                    last.then_inc(S["ctx2_tp"], 1)

            def project_out(b):
                for k in range(2):
                    pe.wait_ge(S["ctx2_evac"], 2 * b + (k + 1))
                    pe.wait_ge(S["att_evac"], 2 * b + START)
                    mm(ps[:, 2 + k, :], wo_sb[:], ctx_t[:, k, :], start=True, stop=True).then_inc(S["att_mm"], 1)

            def turn_attention(b):
                for k in range(2):
                    pe.wait_ge(S["att_evac"], 2 * b + (k + 1) + START)
                    pe.wait_ge(S["x2_ready"], 2 * b + START)
                    for a in range(CB):
                        last = tp(ps[:, 4 + k, a * P:(a + 1) * P], att_t[:, k, a * P:(a + 1) * P], identf[:])
                    last.then_inc(S["att_tp"], 1)

            def turn_norm(b):
                for k in range(2):
                    pe.wait_ge(S["xn_ready"], NCH + 2 * b + (k + 1))
                    pe.wait_ge(S["h_ready"], NCH + 2 * b + START)
                    for a in range(CB):
                        last = tp(ps[:, 6 + k, a * P:(a + 1) * P], xn2[:, k, a, :], identf[:])
                    last.then_inc(S["xt_done"], 1)

            def router_logits(b):
                for k in range(2):
                    pe.wait_ge(S["h_ready"], NCH + 2 * b + (k + 1) + START)
                    for a in range(CB):
                        last = mm(ps[:, k, a * E:(a + 1) * E], h2_t[:, k, a * P:(a + 1) * P], wg_sb[:],
                                  start=True, stop=True)
                    last.then_inc(S["logit_mm"], 1)

            turn_ctx2(0, first=True)
            project_out(0)
            turn_attention(0)
            with pe.Fori(1, B) as b:
                turn_ctx2(b)
                project_out(b)
                turn_norm(b - 1)
                turn_attention(b)
                router_logits(b - 1)
            turn_norm(B - 1)
            router_logits(B - 1)

            def up(i, f, first=False):
                if not first or f >= 2:
                    pe.wait_ge(S["g_done"], NF * i + (f - 1))
                fs, tok = slice(f * P, (f + 1) * P), ds(i * CH, CH)
                for n, (hi, lo) in enumerate(((w1_hi, w1_lo), (w3_hi, w3_lo))):
                    bank = ps[:, 2 * (f % 2) + n, :]
                    mm(bank, hi[:, fs], h2_hi[:, tok], start=True, stop=False)
                    mm(bank, hi[:, fs], h2_lo[:, tok], start=False, stop=False)
                    last = mm(bank, lo[:, fs], h2_hi[:, tok], start=False, stop=True)
                last.then_inc(S["h_banks"], 1)

            def down(i, f):
                fs = slice(f * P, (f + 1) * P)
                if f == 0:
                    pe.wait_ge(S["y_evac"], i + START)
                pe.wait_ge(S["glo_done"], NF * i + (f + 1))
                mm(ps[:, 4, :], w2_hi[:, fs], g_hi[:, f % AHEAD, :], start=f == 0, stop=False)
                mm(ps[:, 4, :], w2_hi[:, fs], g_lo[:, f % AHEAD, :], start=False, stop=False)
                last = mm(ps[:, 4, :], w2_lo[:, fs], g_hi[:, f % AHEAD, :], start=False, stop=f == NF - 1)
                if f == NF - 1:
                    last.then_inc(S["y_mm"], 1)

            def chunk(i, last_chunk=False):
                for f in range(NF):
                    down(i, f)
                    if f + AHEAD < NF:
                        up(i, f + AHEAD)
                    elif not last_chunk:
                        up(i + 1, f + AHEAD - NF)
                pe.wait_ge(S["y_evac"], i + 1 + START)
                pe.wait_ge(S["o_ready"], i + START)
                for a in range(CB):
                    last = tp(ps[:, 5, a * P:(a + 1) * P], y_sb[:, a * P:(a + 1) * P], identf[:])
                last.then_inc(S["y_tp"], 1)

            pe.wait_ge(S["wlo_ready"], B)
            pe.wait_ge(S["h2lo_ready"], NCH + START)
            pe.wait_ge(S["logit_read"], NCH + START)
            pe.wait_ge(S["x2_ready"], NCH + START)
            for f in range(2):
                up(0, f, first=True)
            pe.wait_ge(S["route_chain"], ROUTE_STEPS * B)
            for half in range(2):
                last = tp(ps[:, 5, half * P:(half + 1) * P],
                          expert_w[:, half * 2 * NB:(half + 1) * 2 * NB, :].rearrange("p n e -> p (n e)"), identf[:])
            last.then_inc(S["ewt_mm"], 1)
            for f in range(2, AHEAD):
                up(0, f, first=True)
            with pe.Fori(0, NCH - 1) as i:
                chunk(i)
            chunk(NCH - 1, last_chunk=True)


def constants():
    f32 = np.float32
    fraction = (2 * np.arange(HD // 2) / HD).astype(f32)
    timescale = np.power(f32(1250), fraction).astype(f32)
    angle = (np.arange(L).astype(f32)[None, :] / timescale[:, None]).astype(f32)
    sin, cos = np.sin(angle), np.cos(angle)
    rope = np.stack([np.tile(np.concatenate([cos, cos]), (NH, 1)), np.tile(np.concatenate([-sin, sin]), (NH, 1))], 1)
    row, col = np.arange(P)[:, None], np.arange(P)[None, :]
    mask = np.where(col > row, MASKED, 0.0)
    e = np.arange(E)
    before = np.tile((e[None, :] < e[:, None]).astype(f32)[None], (P, 1, 1))
    return {"rope": rope.astype(f32), "ident": np.eye(P, dtype=f32), "mask_up": mask.astype(f32),
            "before": before}


def kernel(**inputs):
    import concourse.bacc as bacc
    from concourse.bass_utils import run_bass_kernel_spmd

    a = {k: np.asarray(v) for k, v in inputs.items()}
    swap = np.arange(D).reshape(NH, 2, HD // 2)[:, ::-1].reshape(D)
    wq, bq, wk, bk = (a[f"L0_attn_w{n}"] for n in ("q_w", "q_b", "k_w", "k_b"))
    arrays = {
        "x": a["L0_attn_x"],
        "w_in5": np.stack([wq, wq[:, swap], wk, wk[:, swap], a["L0_attn_wv_w"]], axis=1),
        "cols_in": np.stack([bq, bq[swap], bk, bk[swap], a["L0_attn_wo_b"]], axis=1),
        "bv": a["L0_attn_wv_b"],
        "wo": a["L0_attn_wo_w"],
        "wgT": a["L0_ffn_wg"].T,
        "w1T": a["L0_ffn_w1"].reshape(E * I, D).T,
        "w3T": a["L0_ffn_w3"].reshape(E * I, D).T,
        "w2T": a["L0_ffn_w2"].reshape(E, D, I // P, P).transpose(3, 0, 2, 1).reshape(P, E * I),
        "cT": a["L0_c"].T,
        "wmod": a["L0_wmod"],
        **constants(),
    }
    nc = bacc.Bacc("TRN2", target_bir_lowering=False, num_devices=1)
    feeds, args = {}, []
    for name, arr in arrays.items():
        arr = np.ascontiguousarray(arr)
        feeds[f"in_{name}"] = arr
        args.append(nc.dram_tensor(f"in_{name}", arr.shape, mybir.dt.from_np(arr.dtype), kind="ExternalInput").ap())
    args.append(nc.dram_tensor("out_0", (B, L, D), F32, kind="ExternalOutput").ap())
    build(nc, *args)
    return run_bass_kernel_spmd(nc, [feeds], core_ids=[0]).results[0]["out_0"]
```
